# Optimizing a Trainium2 kernel written in Bass

```python
import numpy as np
import jax
import jax.numpy as jnp

def _softmax(x, axis=-1):
    return jax.nn.softmax(x, axis=axis)

def _gelu(x):
    return jax.nn.gelu(x, approximate=True)

def _silu(x):
    return jax.nn.silu(x)

def _sigmoid(x):
    return jax.nn.sigmoid(x)

def _layernorm(x, axis=-1, eps=1e-05):
    m = jnp.mean(x, axis=axis, keepdims=True)
    v = jnp.var(x, axis=axis, keepdims=True)
    return (x - m) / jnp.sqrt(v + eps)

def _scatter_add(tgt, idx, src, axis=0):
    return tgt.at[idx].add(src)

def _segment_sum(src, seg, n):
    return jax.ops.segment_sum(src, seg, n)
kernel_name = 'mk_adj_resnorm_d2_adj_r2_98bf58'

def setup_inputs(seed: int=0):
    np.random.seed(seed)
    _w = jnp.asarray

    def _rec_inputs():
        import jax
        import jax.numpy as jnp
        _gk = jax.random.key(seed)
        x = 0.0002141 + 1 * jax.random.normal(jax.random.fold_in(_gk, 1), (4096, 128), jnp.float32)
        _a = jax.random.bernoulli(jax.random.fold_in(_gk, 2), 0.00390625, (4096, 4096))
        _af = _a.astype(jnp.float32)
        _af = _af * jax.random.uniform(jax.random.fold_in(_gk, 3), (4096, 4096), jnp.float32, 0.05, 1)
        adj = _af
        return (x, adj)
    x, adj = _rec_inputs()

    def _L0_gnn_setup():
        import jax, jax.numpy as jnp
        import numpy as np
        N, F_IN, F_OUT, H, ALPHA = (1536, 128, 128, 8, 0.2)
        D = F_OUT // H
        LN_EPS = 1e-05

        def _xavier(key, shape, fan_in, fan_out):
            lim = np.sqrt(6.0 / (fan_in + fan_out))
            return jax.random.uniform(key, shape, jnp.float32, -lim, lim)
        key = jax.random.key(seed)
        ks = jax.random.split(key, 12)
        x = jax.random.normal(ks[0], (N, F_IN), jnp.float32)
        u = jax.random.uniform(ks[1], (N, N), jnp.float32)
        w = jax.random.uniform(ks[2], (N, N), jnp.float32)
        adj_matrix = jnp.where(u < 0.1, w, 0.0)
        W = _xavier(ks[3], (F_OUT, F_IN), F_IN, F_OUT)
        attn_src = _xavier(ks[4], (H, D), H * D, 1)
        attn_dst = _xavier(ks[5], (H, D), H * D, 1)
        edge_W = _xavier(ks[6], (H, 1), 1, H)
        edge_b = jnp.zeros((H,), jnp.float32)
        fuse_W = _xavier(ks[7], (F_OUT, F_OUT), F_OUT, F_OUT)
        fuse_b = jnp.zeros((F_OUT,), jnp.float32)
        ln_g = jnp.ones((F_OUT,), jnp.float32)
        ln_b = jnp.zeros((F_OUT,), jnp.float32)
        return {'x': x, 'adj_matrix': adj_matrix, 'W': W, 'attn_src': attn_src, 'attn_dst': attn_dst, 'edge_W': edge_W, 'edge_b': edge_b, 'fuse_W': fuse_W, 'fuse_b': fuse_b, 'ln_g': ln_g, 'ln_b': ln_b}
    _L0_gnn_all = _L0_gnn_setup()
    _L0_gnn_in = {k: v for k, v in _L0_gnn_all.items() if k in ('W', 'attn_src', 'attn_dst', 'edge_W', 'edge_b', 'fuse_W', 'fuse_b', 'ln_g', 'ln_b')}
    del _L0_gnn_all

    def _L1_gnn_setup():
        import jax, jax.numpy as jnp
        import numpy as np
        N = 4096
        D = 128
        DENSITY = 0.02
        key = jax.random.key(seed)
        k1, k2, k3, k4 = jax.random.split(key, 4)
        inputs = jax.random.normal(k1, (N, D), dtype=jnp.float32)
        vals = jax.random.uniform(k2, (N, N), dtype=jnp.float32, minval=0.1, maxval=1.0)
        mask = jax.random.uniform(k3, (N, N), dtype=jnp.float32) < DENSITY
        adj = jnp.where(mask, vals, 0.0)
        H_v = 0.1 * jax.random.normal(k4, (D, 1), dtype=jnp.float32)
        return {'inputs': inputs, 'adj': adj, 'H_v': H_v}
    _L1_gnn_all = _L1_gnn_setup()
    _L1_gnn_in = {k: v for k, v in _L1_gnn_all.items() if k in ('H_v',)}
    del _L1_gnn_all
    return {'x': x, 'adj': adj, 'L0_gnn_W': _L0_gnn_in['W'], 'L0_gnn_attn_src': _L0_gnn_in['attn_src'], 'L0_gnn_attn_dst': _L0_gnn_in['attn_dst'], 'L0_gnn_edge_W': _L0_gnn_in['edge_W'], 'L0_gnn_edge_b': _L0_gnn_in['edge_b'], 'L0_gnn_fuse_W': _L0_gnn_in['fuse_W'], 'L0_gnn_fuse_b': _L0_gnn_in['fuse_b'], 'L0_gnn_ln_g': _L0_gnn_in['ln_g'], 'L0_gnn_ln_b': _L0_gnn_in['ln_b'], 'L1_gnn_H_v': _L1_gnn_in['H_v']}

def reference(x, adj, L0_gnn_W, L0_gnn_attn_src, L0_gnn_attn_dst, L0_gnn_edge_W, L0_gnn_edge_b, L0_gnn_fuse_W, L0_gnn_fuse_b, L0_gnn_ln_g, L0_gnn_ln_b, L1_gnn_H_v):
    import jax
    import jax.numpy as jnp

    def _L0_gnn_ref(x, adj_matrix, W, attn_src, attn_dst, edge_W, edge_b, fuse_W, fuse_b, ln_g, ln_b):
        import jax, jax.numpy as jnp
        import numpy as np
        N, F_IN, F_OUT, H, ALPHA = (1536, 128, 128, 8, 0.2)
        D = F_OUT // H
        LN_EPS = 1e-05

        def _xavier(key, shape, fan_in, fan_out):
            lim = np.sqrt(6.0 / (fan_in + fan_out))
            return jax.random.uniform(key, shape, jnp.float32, -lim, lim)
        n = x.shape[0]
        h = (x @ W.T).reshape(n, H, D)
        a_src = jnp.einsum('nhd,hd->nh', h, attn_src)
        a_dst = jnp.einsum('nhd,hd->nh', h, attn_dst)
        attn = a_src[:, None, :] + a_dst[None, :, :]
        attn = attn + adj_matrix[:, :, None] * edge_W[:, 0] + edge_b
        mask = (adj_matrix > 0)[:, :, None]
        attn = jnp.where(mask, attn, -jnp.inf)
        attn = jnp.where(attn >= 0, attn, ALPHA * attn)
        attn = jax.nn.softmax(attn, axis=1)
        h_out = jnp.einsum('ijh,jhd->ihd', attn, h).reshape(n, H * D)
        y = h_out @ fuse_W.T + fuse_b
        mu = jnp.mean(y, axis=-1, keepdims=True)
        var = jnp.mean(jnp.square(y - mu), axis=-1, keepdims=True)
        y = (y - mu) * jax.lax.rsqrt(var + LN_EPS) * ln_g + ln_b
        return jax.nn.relu(y)

    def _L1_gnn_ref(inputs, adj, H_v):
        import jax, jax.numpy as jnp
        import numpy as np
        N = 4096
        D = 128
        DENSITY = 0.02
        scores = jnp.squeeze(inputs @ H_v, -1)
        mask = adj != 0.0
        logits = adj * scores[None, :]
        neg = jnp.asarray(jnp.finfo(logits.dtype).min, logits.dtype)
        logits = jnp.where(mask, logits, neg)
        m = jnp.max(logits, axis=1, keepdims=True)
        e = jnp.where(mask, jnp.exp(logits - m), 0.0)
        s = jnp.sum(e, axis=1, keepdims=True)
        weights = e / jnp.where(s > 0, s, 1.0)
        return weights @ inputs
    x = _layernorm(x + _L0_gnn_ref(x, adj, L0_gnn_W, L0_gnn_attn_src, L0_gnn_attn_dst, L0_gnn_edge_W, L0_gnn_edge_b, L0_gnn_fuse_W, L0_gnn_fuse_b, L0_gnn_ln_g, L0_gnn_ln_b), axis=-1)
    x = _layernorm(x + _L1_gnn_ref(x, adj, L1_gnn_H_v), axis=-1)
    return x

_drawn_inputs = setup_inputs


def setup_inputs(seed=0):
    import zlib

    import numpy as np

    out = dict(_drawn_inputs(seed))
    spreads = {'L0_gnn_edge_b': (0.0, 0.36),
     'L0_gnn_fuse_b': (0.0, 0.1),
     'L0_gnn_ln_g': (1.0, 0.2),
     'L0_gnn_ln_b': (0.0, 0.1)}
    factors = {}
    for name, (base, spread) in spreads.items():
        noise = np.random.default_rng([zlib.crc32(name.encode()), seed]).standard_normal(out[name].shape)
        drawn = base * np.exp(spread * noise) if base else spread * noise
        out[name] = jnp.asarray(drawn.astype(out[name].dtype))
    for name, factor in factors.items():
        out[name] = (out[name] * factor).astype(out[name].dtype)
    return out
```

```python
from contextlib import ExitStack

import concourse.bass as bass
from concourse import mybir

F32 = mybir.dt.float32
U32 = mybir.dt.uint32
F32R = mybir.dt.float32r
ALU = mybir.AluOpType
ACT = mybir.ActivationFunctionType
AX = mybir.AxisListType
RMAX = bass.bass_isa.ReduceOp.max

P = 128
N = 4096
F = 128
H = 8
D = F // H
HP = 32
HG = P // HP
NG = H // HG
NT = N // P
IB = 1024
NB = N // IB
HALF = 512
NH = IB // HALF
TB = IB // P
XW = 132
CH = 512
NC = N // CH
TC = CH // P
ALPHA = 0.2
EPS = 1e-5
NO_EDGE = -float(2.0 ** 100)
W_MIN = 1e-25
QR = HP + H
RING = 8
ES = 4
CONSTS = 10
AGG0 = 2 * NG
SC0 = 2


def gnn_kernel(nc, xT, x, adjT, wT, w, attn, edge, edge_col, fuse, rows, select, pick, ident, out):
    z_rows = nc.dram_tensor("z_rows", [H, N], F32, kind="Internal").ap()
    z_inv_rows = nc.dram_tensor("z_inv_rows", [H, N], F32, kind="Internal").ap()
    with ExitStack() as ctx:
        def sb(name, shape, dt=F32):
            return ctx.enter_context(nc.sbuf_tensor(name, shape, dt))

        def sem(name):
            return ctx.enter_context(nc.semaphore(name))

        adj_in = sb("adj_in", [P, 2, IB])
        pos = sb("pos", [P, IB])
        hi = sb("hi", [P, 2, 2 * IB], F32R)
        lo = sb("lo", [P, 2, IB], F32R)
        fifth = sb("fifth", [P, NT * XW])
        fifth_v = fifth[:, 0:4 * IB].rearrange("p (q n) -> p q n", q=2)
        x1 = fifth[:, :].rearrange("p (t c) -> p t c", c=XW)
        big = sb("big", [P, 2 * H * IB])
        weights = big[:, :].rearrange("p (s h n) -> p s h n", s=2, h=H)
        xT_all = big[:, 0:N]
        pick_in = big[:, N:N + H * P].rearrange("p (h n) -> p h n", h=H)
        q_all = big[0:QR, 2 * N:3 * N]
        y_all = big[:, 0:N]
        sq_all = big[:, N:2 * N]
        x_all = big[:, 2 * N:3 * N]
        e_all = big[:, 3 * N:4 * N].rearrange("p (s n) -> p s n", s=4)
        q_rows = sb("q_rows", [P, N], F32R)
        hid = sb("hid", [P, NT * F])
        agg = sb("agg", [P, NG, N])
        ring = agg[:, :, :].rearrange("p g (s n) -> p (g s) n", n=IB)
        xT_tile = sb("xT_tile", [P, 2, P])
        h_tile = sb("h_tile", [P, 2, H, HP])
        proj = sb("proj", [P, F + H])
        w_sb = sb("w_sb", [P, F])
        attn_sb = sb("attn_sb", [P, 2 * H])
        src_cols = sb("src_cols", [P, QR])
        edge_sb = sb("edge_sb", [P, 2, H])
        col_sb = sb("col_sb", [QR, 2])
        col_w = sb("col_w", [QR, 3])
        w_abs = sb("w_abs", [P, H])
        w_inv = sb("w_inv", [P, H])
        w_sign = sb("w_sign", [P, H], U32)
        w_sgn = sb("w_sgn", [P, H])
        signed_id = sb("signed_id", [P, H, P], F32R)
        pick_sb = sb("pick_sb", [P, H, P], F32R)
        ident_sb = sb("ident_sb", [P, P])
        d_all = sb("d_all", [P, NT * H])
        up_bias = sb("up_bias", [P, NT * H])
        exp_bias = sb("exp_bias", [P, NT * H])
        d_max = sb("d_max", [P, H])
        d_top = sb("d_top", [P, H])
        fuse_sb = sb("fuse_sb", [P, NG, F])
        rows_sb = sb("rows_sb", [P, 4, F])
        sel_sb = sb("sel_sb", [P, P])
        z_sb = sb("z_sb", [P, H * N // P])
        z1_fix = sb("z1_fix", [P, TB])
        agg_n = adj_in
        stat = sb("stat", [P, 8, NT])
        score_top = sb("score_top", [P, 2])

        ps = ctx.enter_context(nc.psum_tensor("ps", [P, 8, HALF], F32))
        acc = ps[:, 0:NG * NH, :].rearrange("p (g b) n -> p g b n", b=NH)
        z_ps = ps[:, NG * NH:8, :].rearrange("p (s b) n -> p s b n", b=NH)

        consts_in = sem("consts_in")
        xT_in = sem("xT_in")
        x_in = sem("x_in")
        adj_arrived = [sem(f"adj_arrived_{q}") for q in range(2)]
        adj_free = sem("adj_free")
        src_dst_mm = sem("src_dst_mm")
        proj_ready = sem("proj_ready")
        xT_tile_ready = sem("xT_tile_ready")
        hid_mm = sem("hid_mm")
        hid_copied = sem("hid_copied")
        hid_ready = sem("hid_ready")
        heads_ready = sem("heads_ready")
        q_mm = sem("q_mm")
        q_scaled = sem("q_scaled")
        q_ready = sem("q_ready")
        vec = sem("vec")
        d_max_ready = sem("d_max_ready")
        d_top_ready = sem("d_top_ready")
        setup_ready = sem("setup_ready")
        h_tile_ready = sem("h_tile_ready")
        no_edge_ready = sem("no_edge_ready")
        pos_ready = sem("pos_ready")
        hi_ready = sem("hi_ready")
        abs_ready = sem("abs_ready")
        lo_ready = sem("lo_ready")
        fifth_ready = sem("fifth_ready")
        fifth_neg_ready = sem("fifth_neg_ready")
        z_mm = sem("z_mm")
        score_ready = sem("score_ready")
        weight_ready = sem("weight_ready")
        agg_mm = sem("agg_mm")
        agg_ready = sem("agg_ready")
        zeroed = sem("zeroed")
        z_out = sem("z_out")
        z_in = sem("z_in")
        z_inv_ready = sem("z_inv_ready")
        z_inv_out = sem("z_inv_out")
        z_inv_in = sem("z_inv_in")
        spread_mm = sem("spread_mm")
        agg_n_ready = sem("agg_n_ready")
        y_mm = sem("y_mm")
        y_ready = sem("y_ready")
        var_ready = sem("var_ready")
        std_ready = sem("std_ready")
        score_max_ready = sem("score_max_ready")
        score_top_ready = sem("score_top_ready")
        x1_ready = sem("x1_ready")
        ring_arrived = [sem(f"ring_arrived_{q}") for q in range(RING)]
        ring_free = sem("ring_free")
        e_raw = sem("e_raw")
        e_ready = sem("e_ready")
        l1_mm = sem("l1_mm")
        l1_z = sem("l1_z")
        l1_out = sem("l1_out")
        out_ready = sem("out_ready")
        stored = sem("stored")

        STEPS = NB * NT

        block = ctx.enter_context(nc.Block())

        @block.sync
        def _(sp):
            sp.dma_start(w_sb[:, :], w).then_inc(consts_in, 16)
            sp.dma_start(attn_sb[:, :], attn).then_inc(consts_in, 16)
            sp.dma_start(proj[:, 0:F], wT).then_inc(consts_in, 16)
            sp.dma_start(edge_sb[:, :, :], edge.partition_broadcast(P)).then_inc(consts_in, 16)
            sp.dma_start(col_sb[:, :], edge_col).then_inc(consts_in, 16)
            sp.dma_start(fuse_sb[:, :, :], fuse).then_inc(consts_in, 16)
            sp.dma_start(rows_sb[:, :, :], rows.partition_broadcast(P)).then_inc(consts_in, 16)
            sp.dma_start(sel_sb[:, :], select).then_inc(consts_in, 16)
            sp.dma_start(ident_sb[:, :], ident).then_inc(consts_in, 16)
            sp.dma_start(pick_in, pick).then_inc(consts_in, 16)
            sp.dma_start(xT_all, xT).then_inc(xT_in, 16)
            with sp.Fori(0, STEPS // 2) as kk:
                for q in range(2):
                    sp.wait_ge(adj_free, kk * 2 + q + 1)
                    sp.dma_start(adj_in[:, q, :], adjT[bass.ds(kk * 2 * P + q * P, P), :]).then_inc(adj_arrived[q], 16)
            sp.wait_ge(adj_free, STEPS + 1)
            sp.dma_start(adj_in[:, 0, :], adjT[0:P, :]).then_inc(adj_arrived[0], 16)
            sp.wait_ge(agg_mm, AGG0 + NG * STEPS)
            sp.dma_start(x_all.rearrange("p (t f) -> p t f", f=F), x.rearrange("(t p) f -> p t f", p=P)).then_inc(x_in, 16)
            sp.wait_ge(agg_ready, 1 + NB * NG * NH)
            for g in range(NG):
                sp.dma_start(z_rows[g * HG:(g + 1) * HG, :], agg[D:P:HP, g, :]).then_inc(z_out, 16)
            sp.wait_ge(z_out, NG * 16)
            sp.dma_start(z_sb[:, :], z_rows.rearrange("h (a b) -> (h a) b", b=H * N // P)).then_inc(z_in, 16)
            sp.wait_ge(z_inv_ready, 1)
            sp.dma_start(z_inv_rows.rearrange("h (a b) -> (h a) b", b=H * N // P), z_sb[:, :]).then_inc(z_inv_out, 16)
            sp.wait_ge(z_inv_out, 16)
            for g in range(NG):
                sp.dma_start(agg[D:P:HP, g, :], z_inv_rows[g * HG:(g + 1) * HG, :]).then_inc(z_inv_in, 16)
            sp.wait_ge(y_ready, 1 + NC)
            with sp.Fori(0, STEPS // RING) as kk:
                for q in range(RING):
                    sp.wait_ge(ring_free, kk * RING + q + 1)
                    sp.dma_start(ring[:, q, :], adjT[bass.ds(kk * (RING * P) + q * P, P), :]).then_inc(ring_arrived[q], 16)
            sp.wait_ge(out_ready, 1)
            sp.dma_start(out.rearrange("(t p) f -> p t f", p=P), sq_all.rearrange("p (t f) -> p t f", f=F)).then_inc(stored, 16)
            sp.wait_ge(stored, 16)

        @block.gpsimd
        def _(pool):
            nc.gpsimd.memset(h_tile[:, :, :, :], 0.0).then_inc(zeroed, 1)
            nc.gpsimd.memset(src_cols[:, :], 0.0).then_inc(zeroed, 1)
            pool.wait_ge(zeroed, 2)
            nc.gpsimd.memset(h_tile[:, :, :, D:D + 1], 1.0).then_inc(zeroed, 1)
            nc.gpsimd.memset(q_rows[:, :].bitcast(F32), 0.0).then_inc(zeroed, 1)
            pool.wait_ge(xT_in, 16)
            with pool.Fori(0, NT // 2) as tt:
                for q in range(2):
                    pool.wait_ge(hid_mm, tt * 2 + q + 1)
                    nc.gpsimd.tensor_copy(xT_tile[:, q, :], xT_all[:, bass.ds(tt * 2 * P + q * P, P)]).then_inc(xT_tile_ready, 1)
            pool.wait_ge(d_max_ready, 1)
            nc.gpsimd.partition_all_reduce(d_top[:, :], d_max[:, :], P, RMAX).then_inc(d_top_ready, 1)
            pool.wait_ge(score_max_ready, 1)
            nc.gpsimd.partition_all_reduce(score_top[:, 1:2], score_top[:, 0:1], P, RMAX).then_inc(score_top_ready, 1)

        @block.tensor
        def _(pe):
            pe.sem_inc(hid_mm, 2)
            pe.sem_inc(agg_mm, AGG0)
            pe.sem_inc(z_mm, H)
            pe.sem_inc(y_mm, 1)
            pe.sem_inc(l1_mm, ES)
            pe.wait_ge(consts_in, CONSTS * 16)
            nc.tensor.matmul(ps[:, 0, 0:2 * H], w_sb[:, :], attn_sb[:, :], start=True, stop=True).then_inc(src_dst_mm, 1)
            pe.wait_ge(proj_ready, 3)
            with pe.Fori(0, NT // 2) as tt:
                for q in range(2):
                    pe.wait_ge(xT_tile_ready, tt * 2 + q + 1)
                    pe.wait_ge(hid_ready, tt * 2 + q + 1)
                    nc.tensor.matmul(ps[:, q, 0:F + H], xT_tile[:, q, :], proj[:, :], start=True, stop=True).then_inc(hid_mm, 1)
            for c in range(N // HALF):
                if c >= 4:
                    pe.wait_ge(q_scaled, c - 3)
                nc.tensor.matmul(ps[0:QR, 4 + c % 4, :], src_cols[:, :], xT_all[:, c * HALF:(c + 1) * HALF],
                                 start=True, stop=True).then_inc(q_mm, 1)
            sign = [pe.snap(nc.tensor.value_load(w_sign[0:1, h:h + 1], min_val=0, max_val=1) * IB) for h in range(H)]
            pe.wait_ge(hid_ready, NT + 2)
            pe.wait_ge(zeroed, 3)
            pe.wait_ge(q_ready, 3)
            pe.wait_ge(setup_ready, 1)
            with pe.Fori(0, NB) as ib:

                def sums(k, q, h):
                    s = h % 2
                    if h == 0:
                        pe.wait_ge(abs_ready, k + 1)
                        pe.wait_ge(lo_ready, k + 1)
                    pe.wait_ge(score_ready, k * H + h + 1)
                    for b in range(NH):
                        nc.tensor.matmul(z_ps[:, s, b, :], signed_id[:, h, :], hi[:, q, bass.ds(sign[h] + b * HALF, HALF)], start=True, stop=False)
                        nc.tensor.matmul(z_ps[:, s, b, :], signed_id[:, h, :], lo[:, q, b * HALF:(b + 1) * HALF], start=False, stop=False)
                    for b in range(NH):
                        last = nc.tensor.matmul(z_ps[:, s, b, :], pick_sb[:, h, :], q_rows[:, bass.ds(ib * IB + b * HALF, HALF)], start=False, stop=True)
                    last.then_inc(z_mm, 1)

                def gather(k, q, g, b, start, stop):
                    if b == 0:
                        pe.wait_ge(h_tile_ready, k + 1)
                        pe.wait_ge(weight_ready, k * H + (g + 1) * HG)
                    for c in range(HG):
                        last = nc.tensor.matmul(acc[c * HP:(c + 1) * HP, g, b, :], h_tile[:, q, g * HG + c, :],
                                                weights[:, q, g * HG + c, b * HALF:(b + 1) * HALF],
                                                start=start, stop=stop)
                    if b == NH - 1:
                        last.then_inc(agg_mm, 1)

                def step(k, q, start=False, stop=False, second=False):
                    for h in range(H):
                        sums(k, q, h)
                        if h == H // 2 and start:
                            pe.wait_ge(agg_ready, 1 + ib * (NG * NH))
                        if h % 2 and h < H // 2 and not start:
                            gather(k - 1, 1 - q, 1, h // 2, second, False)
                        if h % 2 and h > H // 2:
                            gather(k, q, 0, h // 2 - NH, start, stop)
                    if stop:
                        for b in range(NH):
                            gather(k, q, 1, b, False, True)

                step(ib * NT, 0, start=True)
                step(ib * NT + 1, 1, second=True)
                with pe.Fori(1, NT // 2 - 1) as jj:
                    for q in range(2):
                        step(ib * NT + jj * 2 + q, q)
                step(ib * NT + NT - 2, 0)
                step(ib * NT + NT - 1, 1, stop=True)
            pe.wait_ge(z_inv_in, NG * 16)
            with pe.Fori(0, NC) as c:
                pe.wait_ge(agg_n_ready, c + 1)
                for g in range(NG):
                    last = nc.tensor.matmul(ps[:, g, :], sel_sb[:, :], agg[:, g, bass.ds(c * CH, CH)], start=True, stop=True)
                last.then_inc(spread_mm, 1)
                pe.wait_ge(agg_n_ready, c + 2)
                pe.wait_ge(y_ready, c + 1)
                for t in range(TC):
                    for g in range(NG):
                        last = nc.tensor.matmul(ps[:, 4, t * F:(t + 1) * F], agg_n[:, g, t * P:(t + 1) * P],
                                                fuse_sb[:, g, :], start=(g == 0), stop=(g == NG - 1))
                last.then_inc(y_mm, 1)
            pe.wait_ge(x1_ready, 1)
            with pe.Fori(0, NB) as ib:
                pe.wait_ge(l1_out, 1 + ib * TB)

                def step1(k, jt, q, start, stop):
                    pe.wait_ge(e_ready, k + 1)
                    for t in range(TB):
                        last = nc.tensor.matmul(ps[:, t, 0:F + 1], e_all[:, q % ES, t * P:(t + 1) * P],
                                                fifth[:, bass.ds(jt * XW, F + 1)], start=start, stop=stop)
                    last.then_inc(l1_mm, 1)

                for q in range(ES):
                    step1(ib * NT + q, q, q, q == 0, False)
                with pe.Fori(1, NT // ES - 1) as jj:
                    for q in range(ES):
                        step1(ib * NT + jj * ES + q, jj * ES + q, q, False, False)
                for q in range(ES):
                    step1(ib * NT + NT - ES + q, NT - ES + q, q, False, q == ES - 1)

        @block.scalar
        def _(act):
            act.sem_inc(hid_ready, 2)
            act.sem_inc(agg_ready, 1)
            with act.Fori(0, NT // 2) as tt:
                for q in range(2):
                    act.wait_ge(hid_mm, 2 + tt * 2 + q + 1)
                    nc.scalar.copy(hid[:, bass.ds((tt * 2 + q) * F, F)], ps[:, q, 0:F]).then_inc(hid_copied, 1)
                    nc.scalar.copy(d_all[:, bass.ds((tt * 2 + q) * H, H)], ps[:, q, F:F + H]).then_inc(hid_copied, 1)
                    act.wait_ge(hid_copied, (tt * 2 + q + 1) * 2)
                    act.sem_inc(hid_ready, 1)
            act.wait_ge(heads_ready, 1)
            for c in range(N // HALF):
                act.wait_ge(q_mm, c + 1)
                nc.scalar.activation(q_all[:, c * HALF:(c + 1) * HALF], ps[0:QR, 4 + c % 4, :], ACT.Identity,
                                     scale=col_w[:, 1:2], bias=col_w[:, 2:3]).then_inc(q_scaled, 1)

            act.wait_ge(pos_ready, 2)
            act.wait_ge(setup_ready, 1)
            nc.scalar.copy(hi[:, 0, 0:IB], pos[:, :]).then_inc(hi_ready, 1)
            nc.scalar.activation(hi[:, 0, IB:2 * IB], pos[:, :], ACT.Abs).then_inc(abs_ready, 1)
            nc.scalar.mul(fifth_v[:, 0, 0:IB], pos[:, :], ALPHA).then_inc(fifth_ready, 1)
            act.wait_ge(zeroed, 3)
            with act.Fori(0, NB) as ib:
                with act.Fori(0, NT // 2) as jj:
                    for q in range(2):
                        k = ib * NT + jj * 2 + q
                        jt = jj * 2 + q
                        act.wait_ge(agg_mm, k * NG + NG)
                        nc.scalar.copy(h_tile[:, q, :, 0:D], hid[:, bass.ds(jt * F, F)].rearrange("p (h d) -> p h d", h=H)).then_inc(h_tile_ready, 1)
                        for h in range(H):
                            act.wait_ge(score_ready, SC0 + k * H + h + 1)
                            nc.scalar.activation(weights[:, q, h, :], weights[:, q, h, :], ACT.Exp,
                                                 scale=w_abs[:, h:h + 1], bias=exp_bias[:, bass.ds(jt * H + h, 1)]).then_inc(weight_ready, 1)
                            if h == 3:
                                act.wait_ge(pos_ready, k + 3)
                                act.wait_ge(z_mm, k * H + H)
                                nc.scalar.copy(hi[:, 1 - q, 0:IB], pos[:, :]).then_inc(hi_ready, 1)
                            if h == 4:
                                nc.scalar.activation(hi[:, 1 - q, IB:2 * IB], pos[:, :], ACT.Abs).then_inc(abs_ready, 1)
                            if h == 5:
                                nc.scalar.mul(fifth_v[:, 1 - q, 0:IB], pos[:, :], ALPHA).then_inc(fifth_ready, 1)
                act.wait_ge(agg_mm, AGG0 + ib * (NG * NT) + NG * NT)
                for g in range(NG):
                    for b in range(NH):
                        nc.scalar.copy(agg[:, g, bass.ds(ib * IB + b * HALF, HALF)], acc[:, g, b, :]).then_inc(agg_ready, 1)
            for n in range(3):
                if n == 2:
                    act.wait_ge(score_top_ready, 1)
                    act.wait_ge(x1_ready, 1)
                    with act.Fori(0, NB) as ib:
                        with act.Fori(0, NT // RING) as jj:
                            for q in range(RING):
                                jt = jj * RING + q
                                k = ib * NT + jt
                                act.wait_ge(l1_mm, k + 1)
                                act.wait_ge(ring_arrived[q], ib * (16 * NT // RING) + jj * 16 + 16)
                                nc.scalar.activation(e_all[:, q % ES, :], ring[:, q, :], ACT.Exp,
                                                     scale=stat[:, 4, bass.ds(jt, 1)], bias=stat[:, 5, 0:1]).then_inc(e_raw, 1)
                act.wait_ge(var_ready, n + 1)
                nc.scalar.sqrt(stat[:, 3, :], stat[:, 2, :]).then_inc(std_ready, 1)

        @block.vector
        def _(dve):
            chain = [0]

            def tick(ins):
                chain[0] += 1
                return ins.then_inc(vec, 1)

            def link(ins):
                tick(ins)
                dve.wait_ge(vec, chain[0])

            dve.sem_inc(adj_free, 2)
            dve.sem_inc(pos_ready, 1)
            dve.sem_inc(score_ready, SC0)
            dve.sem_inc(agg_n_ready, 1)
            dve.sem_inc(y_ready, 1)
            dve.sem_inc(ring_free, RING)
            dve.sem_inc(l1_out, 1)
            dve.wait_ge(consts_in, CONSTS * 16)
            dve.wait_ge(zeroed, 2)
            dve.wait_ge(src_dst_mm, 1)
            nc.vector.tensor_copy(proj[:, F:F + H], ps[:, 0, H:2 * H]).then_inc(proj_ready, 1)
            nc.vector.tensor_copy(src_cols[:, 0:H], ps[:, 0, 0:H]).then_inc(proj_ready, 1)
            nc.vector.tensor_copy(src_cols[:, HP:HP + H], ps[:, 0, 0:H]).then_inc(proj_ready, 1)
            tick(nc.vector.tensor_scalar(col_w[:, 0:1].bitcast(U32), col_sb[:, 0:1].bitcast(U32), 0x7FFFFFFF, None, ALU.bitwise_and))
            tick(nc.vector.tensor_scalar(w_abs[:, :].bitcast(U32), edge_sb[:, 0, :].bitcast(U32), 0x7FFFFFFF, None, ALU.bitwise_and))
            link(nc.vector.tensor_scalar(w_sign[:, :], edge_sb[:, 0, :].bitcast(U32), 31, None, ALU.logical_shift_right))
            tick(nc.vector.tensor_scalar(col_w[:, 0:1], col_w[:, 0:1], W_MIN, None, ALU.max))
            tick(nc.vector.tensor_scalar(w_abs[:, :], w_abs[:, :], W_MIN, None, ALU.max))
            link(nc.vector.tensor_copy(w_sgn[:, :], w_sign[:, :]))
            tick(nc.vector.reciprocal(col_w[:, 1:2], col_w[:, 0:1]))
            tick(nc.vector.reciprocal(w_inv[:, :], w_abs[:, :]))
            link(nc.vector.tensor_scalar(w_sgn[:, :], w_sgn[:, :], -2.0, 1.0, ALU.mult, ALU.add))
            link(nc.vector.tensor_scalar(col_w[:, 1:2], col_w[:, 1:2], 1.0 - ALPHA, None, ALU.mult))
            nc.vector.tensor_tensor(col_w[:, 2:3], col_sb[:, 1:2], col_w[:, 1:2], ALU.mult).then_inc(heads_ready, 1)
            for h in range(H):
                tick(nc.vector.tensor_scalar(signed_id[:, h, :], ident_sb[:, :], w_sgn[:, h:h + 1], None, ALU.mult))
            link(nc.vector.tensor_copy(pick_sb[:, :, :], pick_in))
            sign = [dve.snap(nc.vector.value_load(w_sign[0:1, h:h + 1], min_val=0, max_val=1) * IB) for h in range(H)]
            dve.wait_ge(q_scaled, N // HALF)
            dve.wait_ge(zeroed, 4)
            nc.vector.tensor_copy(q_rows[0:QR, :], q_all).then_inc(q_ready, 1)
            dve.wait_ge(q_ready, 1)
            nc.vector.tensor_tensor(q_rows[HP:QR, :], q_all[HP:QR, :], q_rows[HP:QR, :].bitcast(F32), ALU.subtract).then_inc(q_ready, 2)
            dve.wait_ge(hid_ready, NT + 2)
            nc.vector.tensor_reduce(d_max[:, :], d_all[:, :].rearrange("p (t h) -> p h t", h=H), AX.X, ALU.max).then_inc(d_max_ready, 1)
            d_v = d_all[:, :].rearrange("p (t h) -> p t h", h=H)
            tick(nc.vector.scalar_tensor_tensor(out=up_bias[:, :].rearrange("p (t h) -> p t h", h=H), in0=d_v, scalar=1.0 - ALPHA,
                                                in1=w_inv[:, :].unsqueeze(1).to_broadcast([P, NT, H]), op0=ALU.mult, op1=ALU.mult))
            dve.wait_ge(d_top_ready, 1)
            link(nc.vector.scalar_tensor_tensor(out=exp_bias[:, :].rearrange("p (t h) -> p t h", h=H), in0=d_v, scalar=ALPHA,
                                                in1=d_top[:, :].unsqueeze(1).to_broadcast([P, NT, H]), op0=ALU.mult, op1=ALU.subtract))
            dve.sem_inc(setup_ready, 1)

            def no_edges(k, q):
                nc.vector.tensor_scalar(pos[:, :], adj_in[:, q, :], 0.0, NO_EDGE, ALU.is_le, ALU.mult).then_inc(no_edge_ready, 1)

            def masked(k, q):
                dve.wait_ge(no_edge_ready, k + 1)
                nc.vector.tensor_tensor(pos[:, :], adj_in[:, q, :], pos[:, :], ALU.add).then_inc(pos_ready, 1)
                dve.wait_ge(pos_ready, k + 2)
                dve.sem_inc(adj_free, 1)

            def rest(k, q):
                dve.wait_ge(hi_ready, k + 1)
                nc.vector.tensor_tensor(lo[:, q, :], pos[:, :], hi[:, q, 0:IB].bitcast(F32), ALU.subtract).then_inc(lo_ready, 1)

            def negative(k, q):
                dve.wait_ge(fifth_ready, k + 1)
                nc.vector.tensor_scalar(fifth_v[:, q, IB:2 * IB].bitcast(U32), fifth_v[:, q, 0:IB].bitcast(U32),
                                        0x80000000, None, ALU.bitwise_or).then_inc(fifth_neg_ready, 1)

            dve.wait_ge(adj_arrived[0], 16)
            no_edges(0, 0)
            masked(0, 0)
            rest(0, 0)
            negative(0, 0)
            with dve.Fori(0, NB) as ib:
                with dve.Fori(0, NT // 2) as jj:
                    for q in range(2):
                        jt = jj * 2 + q
                        k = ib * NT + jt
                        dve.wait_ge(fifth_neg_ready, k + 1)
                        for h in range(H):
                            if h % HG == 0:
                                dve.wait_ge(agg_mm, k * NG + h // HG + 1)
                            dve.wait_ge(z_mm, H + k * H + h + 1)
                            nc.vector.scalar_tensor_tensor(out=weights[:, q, h, :], in0=z_ps[:, h % 2, :, :].rearrange("p b n -> p (b n)"),
                                                           scalar=up_bias[:, bass.ds(jt * H + h, 1)],
                                                           in1=fifth_v[:, q, bass.ds(sign[h], IB)],
                                                           op0=ALU.add, op1=ALU.max).then_inc(score_ready, 1)
                            if h == 1:
                                dve.wait_ge(adj_arrived[1 - q], ib * (8 * NT) + jj * 16 + 16 * (1 + q))
                                dve.wait_ge(abs_ready, k + 1)
                                dve.wait_ge(lo_ready, k + 1)
                                no_edges(k + 1, 1 - q)
                            if h == 3:
                                masked(k + 1, 1 - q)
                            if h == 5:
                                rest(k + 1, 1 - q)
                            if h == 7:
                                negative(k + 1, 1 - q)

            dve.wait_ge(z_in, 16)
            nc.vector.reciprocal(z_sb[:, :], z_sb[:, :]).then_inc(z_inv_ready, 1)
            with dve.Fori(0, NC) as c:
                dve.wait_ge(spread_mm, c + 1)
                dve.wait_ge(y_mm, c + 1)
                nc.vector.tensor_tensor(agg_n[:, :, 0:CH], agg[:, :, bass.ds(c * CH, CH)], ps[:, 0:NG, :], ALU.mult).then_inc(agg_n_ready, 1)
                dve.wait_ge(y_mm, c + 2)
                nc.vector.tensor_tensor(y_all[:, bass.ds(c * CH, CH)].rearrange("p (t f) -> p t f", f=F),
                                        ps[:, 4, :].rearrange("p (t f) -> p t f", f=F),
                                        rows_sb[:, 0, :].unsqueeze(1).to_broadcast([P, TC, F]), ALU.add).then_inc(y_ready, 1)
            dve.wait_ge(y_ready, 1 + NC)

            def tiles(v):
                return v.rearrange("p (t f) -> p t f", f=F)

            def wide(v):
                return v.unsqueeze(2).to_broadcast([P, NT, F])

            def row(n):
                return rows_sb[:, n, :].unsqueeze(1).to_broadcast([P, NT, F])

            def normalise(dst, n):
                link(nc.vector.tensor_reduce(stat[:, 0, :], tiles(y_all), AX.X, ALU.add))
                link(nc.vector.tensor_scalar(stat[:, 0, :], stat[:, 0, :], 1.0 / F, None, ALU.mult))
                link(nc.vector.tensor_tensor(tiles(y_all), tiles(y_all), wide(stat[:, 0, :]), ALU.subtract))
                link(nc.vector.tensor_tensor(sq_all, y_all, y_all, ALU.mult))
                link(nc.vector.tensor_reduce(stat[:, 1, :], tiles(sq_all), AX.X, ALU.add))
                nc.vector.tensor_scalar(stat[:, 2, :], stat[:, 1, :], 1.0 / F, EPS, ALU.mult, ALU.add).then_inc(var_ready, 1)
                dve.wait_ge(std_ready, n)
                link(nc.vector.reciprocal(stat[:, 6, :], stat[:, 3, :]))
                return nc.vector.tensor_tensor(dst, tiles(y_all), wide(stat[:, 6, :]), ALU.mult)

            link(normalise(tiles(y_all), 1))
            link(nc.vector.tensor_tensor(tiles(y_all), tiles(y_all), row(1), ALU.mult))
            link(nc.vector.tensor_tensor(tiles(y_all), tiles(y_all), row(2), ALU.add))
            dve.wait_ge(x_in, 16)
            link(nc.vector.scalar_tensor_tensor(out=y_all, in0=y_all, scalar=0.0, in1=x_all, op0=ALU.max, op1=ALU.add))
            link(normalise(x1[:, :, 0:F], 2))
            link(nc.vector.memset(x1[:, :, F:F + 1], 1.0))
            link(nc.vector.tensor_tensor(tiles(sq_all), x1[:, :, 0:F], row(3), ALU.mult))
            link(nc.vector.tensor_reduce(stat[:, 4, :], tiles(sq_all), AX.X, ALU.add))
            nc.vector.tensor_reduce(score_top[:, 0:1], stat[:, 4, :], AX.X, ALU.max).then_inc(score_max_ready, 1)
            dve.wait_ge(score_top_ready, 1)
            nc.vector.tensor_scalar(stat[:, 5, 0:1], score_top[:, 1:2], 0.0, -1.0, ALU.max, ALU.mult).then_inc(x1_ready, 1)
            with dve.Fori(0, NB) as ib:
                with dve.Fori(0, NT // RING) as jj:
                    for q in range(RING):
                        k = ib * NT + jj * RING + q
                        dve.wait_ge(e_raw, k + 1)
                        nc.vector.scalar_tensor_tensor(out=e_all[:, q % ES, :], in0=ring[:, q, :], scalar=0.0, in1=e_all[:, q % ES, :],
                                                       op0=ALU.not_equal, op1=ALU.mult).then_inc(e_ready, 1)
                        dve.wait_ge(e_ready, k + 1)
                        dve.sem_inc(ring_free, 1)
                dve.wait_ge(l1_mm, ES + ib * NT + NT)
                z1 = ps[:, :, F:F + 1].rearrange("p t o -> p (t o)")
                nc.vector.tensor_scalar(z1_fix[:, :], z1, 0.0, None, ALU.is_equal).then_inc(l1_z, 1)
                dve.wait_ge(l1_z, ib * 3 + 1)
                nc.vector.tensor_tensor(z1_fix[:, :], z1_fix[:, :], z1, ALU.add).then_inc(l1_z, 1)
                dve.wait_ge(l1_z, ib * 3 + 2)
                nc.vector.reciprocal(z1_fix[:, :], z1_fix[:, :]).then_inc(l1_z, 1)
                dve.wait_ge(l1_z, ib * 3 + 3)
                for t in range(TB):
                    nc.vector.scalar_tensor_tensor(out=y_all[:, bass.ds(ib * IB + t * F, F)], in0=ps[:, t, 0:F], scalar=z1_fix[:, t:t + 1],
                                                   in1=fifth[:, bass.ds(ib * (TB * XW) + t * XW, F)], op0=ALU.mult, op1=ALU.add).then_inc(l1_out, 1)
            dve.wait_ge(l1_out, 1 + NB * TB)
            normalise(tiles(sq_all), 3).then_inc(out_ready, 1)


def kernel(x, adj, L0_gnn_W, L0_gnn_attn_src, L0_gnn_attn_dst, L0_gnn_edge_W, L0_gnn_edge_b, L0_gnn_fuse_W,
           L0_gnn_fuse_b, L0_gnn_ln_g, L0_gnn_ln_b, L1_gnn_H_v):
    import numpy as np
    import concourse.bacc as bacc
    from concourse import mybir as _mybir
    from concourse.bass_utils import run_bass_kernel_spmd

    x, adj, w, fuse_w = (np.asarray(a) for a in (x, adj, L0_gnn_W, L0_gnn_fuse_W))
    adj_t = adj.T.reshape(NT, P, NB, IB).transpose(2, 0, 1, 3).reshape(NB * NT * P, IB)
    attn = np.zeros((F, 2 * H), x.dtype)
    for h in range(H):
        attn[h * D:(h + 1) * D, h] = np.asarray(L0_gnn_attn_src)[h]
        attn[h * D:(h + 1) * D, H + h] = np.asarray(L0_gnn_attn_dst)[h]
    fuse = np.zeros((HG, HP, NG, F), x.dtype)
    fuse[:, 0:D] = fuse_w.T.reshape(NG, HG, D, F).transpose(1, 2, 0, 3)
    select = np.zeros((P, P), x.dtype)
    for c in range(HG):
        select[c * HP + D, c * HP:(c + 1) * HP] = 1.0
    rows = np.stack([np.asarray(a).reshape(F) for a in (L0_gnn_fuse_b, L0_gnn_ln_g, L0_gnn_ln_b, L1_gnn_H_v)])
    edge = np.stack([np.asarray(L0_gnn_edge_W).reshape(H), np.asarray(L0_gnn_edge_b).reshape(H)])
    edge_col = np.zeros((HP + H, 2), x.dtype)
    edge_col[0:H] = edge_col[HP:HP + H] = edge.T
    pick = np.zeros((P, H, P), x.dtype)
    for h in range(H):
        pick[h, h] = pick[HP + h, h] = 1.0
    arrays = {"xT": x.T, "x": x, "adjT": adj_t, "wT": w.T, "w": w, "attn": attn, "edge": edge, "edge_col": edge_col,
              "fuse": fuse.reshape(P, NG, F), "rows": rows, "select": select,
              "pick": pick, "ident": np.eye(P, dtype=x.dtype)}
    arrays = {n: np.ascontiguousarray(a) for n, a in arrays.items()}
    nc = bacc.Bacc("TRN2", target_bir_lowering=False, num_devices=1)
    args = [nc.dram_tensor(n, a.shape, _mybir.dt.from_np(a.dtype), kind="ExternalInput").ap() for n, a in arrays.items()]
    args.append(nc.dram_tensor("out", x.shape, _mybir.dt.from_np(x.dtype), kind="ExternalOutput").ap())
    gnn_kernel(nc, *args)
    return run_bass_kernel_spmd(nc, [arrays], core_ids=[0]).results[0]["out"]
```

```python
from contextlib import ExitStack

import concourse.bass as bass
from concourse import mybir

F32 = mybir.dt.float32
U32 = mybir.dt.uint32
F32R = mybir.dt.float32r
ALU = mybir.AluOpType
ACT = mybir.ActivationFunctionType
AX = mybir.AxisListType
RMAX = bass.bass_isa.ReduceOp.max

P = 128
N = 4096
F = 128
H = 8
D = F // H
HP = 32
HG = P // HP
NG = H // HG
NT = N // P
IB = 1024
NB = N // IB
HALF = 512
NH = IB // HALF
TB = IB // P
XW = 132
CH = 512
NC = N // CH
TC = CH // P
ALPHA = 0.2
EPS = 1e-5
NO_EDGE = -float(2.0 ** 100)
W_MIN = 1e-25
QR = HP + H
RING = 8
ES = 4
CONSTS = 10
Z_LOW = 1e-25
Z_HIGH = 1e30
MASKED = -1e30
FOLDS = 7
AGG0 = 2 * NG
SC0 = 2


def gnn_kernel(nc, xT, x, adjT, wT, w, attn, edge, edge_col, fuse, rows, select, pick, ident, out):
    z_rows = nc.dram_tensor("z_rows", [H, N], F32, kind="Internal").ap()
    z_inv_rows = nc.dram_tensor("z_inv_rows", [H, N], F32, kind="Internal").ap()
    q_dram = nc.dram_tensor("q_dram", [QR, N], F32, kind="Internal").ap()
    sums_dram = nc.dram_tensor("sums_dram", [H * HP, N], F32, kind="Internal").ap()
    top_dram = nc.dram_tensor("top_dram", [1, IB], F32, kind="Internal").ap()
    with ExitStack() as ctx:
        def sb(name, shape, dt=F32):
            return ctx.enter_context(nc.sbuf_tensor(name, shape, dt))

        def sem(name):
            return ctx.enter_context(nc.semaphore(name))

        adj_in = sb("adj_in", [P, 2, IB])
        pos = sb("pos", [P, IB])
        hi = sb("hi", [P, 2, 2 * IB], F32R)
        lo = sb("lo", [P, 2, IB], F32R)
        fifth = sb("fifth", [P, NT * XW])
        fifth_v = fifth[:, 0:4 * IB].rearrange("p (q n) -> p q n", q=2)
        x1 = fifth[:, :].rearrange("p (t c) -> p t c", c=XW)
        big = sb("big", [P, 2 * H * IB])
        weights = big[:, :].rearrange("p (s h n) -> p s h n", s=2, h=H)
        xT_all = big[:, 0:N]
        pick_in = big[:, N:N + H * P].rearrange("p (h n) -> p h n", h=H)
        q_all = big[0:QR, 2 * N:3 * N]
        y_all = big[:, 0:N]
        sq_all = big[:, N:2 * N]
        x_all = big[:, 2 * N:3 * N]
        e_all = big[:, 3 * N:4 * N].rearrange("p (s n) -> p s n", s=4)
        q_rows = sb("q_rows", [P, N], F32R)
        hid = sb("hid", [P, NT * F])
        agg = sb("agg", [P, NG, N])
        ring = agg[:, :, :].rearrange("p g (s n) -> p (g s) n", n=IB)
        xT_tile = sb("xT_tile", [P, 2, P])
        h_tile = sb("h_tile", [P, 2, H, HP])
        proj = sb("proj", [P, F + H])
        w_sb = sb("w_sb", [P, F])
        attn_sb = sb("attn_sb", [P, 2 * H])
        src_cols = sb("src_cols", [P, QR])
        edge_sb = sb("edge_sb", [P, 2, H])
        col_sb = sb("col_sb", [QR, 2])
        col_w = sb("col_w", [QR, 3])
        w_abs = sb("w_abs", [P, H])
        w_inv = sb("w_inv", [P, H])
        w_sign = sb("w_sign", [P, H], U32)
        w_sgn = sb("w_sgn", [P, H])
        signed_id = sb("signed_id", [P, H, P], F32R)
        pick_sb = sb("pick_sb", [P, H, P], F32R)
        ident_sb = sb("ident_sb", [P, P])
        d_all = sb("d_all", [P, NT * H])
        up_bias = sb("up_bias", [P, NT * H])
        exp_bias = sb("exp_bias", [P, NT * H])
        d_max = sb("d_max", [P, H])
        d_top = sb("d_top", [P, H])
        fuse_sb = sb("fuse_sb", [P, NG, F])
        rows_sb = sb("rows_sb", [P, 4, F])
        sel_sb = sb("sel_sb", [P, P])
        z_sb = sb("z_sb", [P, H * N // P])
        z1_fix = sb("z1_fix", [P, TB])
        agg_n = adj_in
        stat = sb("stat", [P, 8, NT])
        score_top = sb("score_top", [P, 2])
        z1_all = sb("z1_all", [P, NT])
        in_range = sb("in_range", [P, 2, 2])
        row_x = ring[:, 0, :]
        row_rest = ring[:, 1, :]
        top_x = ring[:, 2, :]
        logit_x = ring[:, 3, :]
        masked_x = ring[:, 4, :]
        fold_x = ring[:, 5, :]
        row_top = ring[:, 6, :]
        acc_x = (ring[0:HP, 7, :], sq_all[:, 0:TB * XW].rearrange("p (t c) -> p t c", c=XW)[:, :, 0:F + 1])

        ps = ctx.enter_context(nc.psum_tensor("ps", [P, 8, HALF], F32))
        acc = ps[:, 0:NG * NH, :].rearrange("p (g b) n -> p g b n", b=NH)
        z_ps = ps[:, NG * NH:8, :].rearrange("p (s b) n -> p s b n", b=NH)

        consts_in = sem("consts_in")
        xT_in = sem("xT_in")
        x_in = sem("x_in")
        adj_arrived = [sem(f"adj_arrived_{q}") for q in range(2)]
        src_dst_mm = sem("src_dst_mm")
        proj_ready = sem("proj_ready")
        xT_tile_ready = sem("xT_tile_ready")
        hid_mm = sem("hid_mm")
        hid_copied = sem("hid_copied")
        hid_ready = sem("hid_ready")
        heads_ready = sem("heads_ready")
        q_mm = sem("q_mm")
        q_scaled = sem("q_scaled")
        q_ready = sem("q_ready")
        vec = sem("vec")
        d_max_ready = sem("d_max_ready")
        d_top_ready = sem("d_top_ready")
        setup_ready = sem("setup_ready")
        h_tile_ready = sem("h_tile_ready")
        no_edge_ready = sem("no_edge_ready")
        pos_ready = sem("pos_ready")
        hi_ready = sem("hi_ready")
        abs_ready = sem("abs_ready")
        lo_ready = sem("lo_ready")
        fifth_ready = sem("fifth_ready")
        fifth_neg_ready = sem("fifth_neg_ready")
        z_mm = sem("z_mm")
        score_ready = sem("score_ready")
        weight_ready = sem("weight_ready")
        agg_mm = sem("agg_mm")
        agg_ready = sem("agg_ready")
        zeroed = sem("zeroed")
        z_out = sem("z_out")
        z_in = sem("z_in")
        z_inv_ready = sem("z_inv_ready")
        z_inv_out = sem("z_inv_out")
        z_inv_in = sem("z_inv_in")
        spread_mm = sem("spread_mm")
        agg_n_ready = sem("agg_n_ready")
        y_mm = sem("y_mm")
        y_ready = sem("y_ready")
        var_ready = sem("var_ready")
        std_ready = sem("std_ready")
        score_max_ready = sem("score_max_ready")
        score_top_ready = sem("score_top_ready")
        x1_ready = sem("x1_ready")
        ring_arrived = [sem(f"ring_arrived_{q}") for q in range(RING)]
        e_raw = sem("e_raw")
        e_ready = sem("e_ready")
        l1_mm = sem("l1_mm")
        l1_z = sem("l1_z")
        l1_out = sem("l1_out")
        out_ready = sem("out_ready")
        stored = sem("stored")
        bad_ready = [sem(f"bad_ready_{n}") for n in range(2)]
        any_bad_ready = [sem(f"any_bad_ready_{n}") for n in range(2)]
        x_rows_in = sem("x_rows_in")
        x_q_out = sem("x_q_out")
        x_adj_in = [sem(f"x_adj_in_{n}") for n in range(2)]
        x_adj_used = [sem(f"x_adj_used_{n}") for n in range(2)]
        x_top_ready = [sem(f"x_top_ready_{n}") for n in range(2)]
        x_half_in = [sem(f"x_half_in_{n}") for n in range(2)]
        x_top_out = [sem(f"x_top_out_{n}") for n in range(2)]
        x_row_top_in = [sem(f"x_row_top_in_{n}") for n in range(2)]
        x_h_ready = sem("x_h_ready")
        x_logit_ready = [sem(f"x_logit_ready_{n}") for n in range(2)]
        x_exp_ready = [sem(f"x_exp_ready_{n}") for n in range(2)]
        x_weight_ready = [sem(f"x_weight_ready_{n}") for n in range(2)]
        x_mm = [sem(f"x_mm_{n}") for n in range(2)]
        x_sums_ready = [sem(f"x_sums_ready_{n}") for n in range(2)]
        x_sums_out = sem("x_sums_out")
        x_agg_in = sem("x_agg_in")
        x_z_out = sem("x_z_out")
        x_z_in = sem("x_z_in")
        x_vec = [sem(f"x_vec_{n}") for n in range(2)]
        XH = (H, 1)

        def any_bad(engine, n):
            return engine.value_load(in_range[0:1, n, 1:2].bitcast(U32), min_val=0, max_val=0x3F800000)

        STEPS = NB * NT

        block = ctx.enter_context(nc.Block())

        @block.sync
        def _(sp):
            sp.dma_start(w_sb[:, :], w).then_inc(consts_in, 16)
            sp.dma_start(attn_sb[:, :], attn).then_inc(consts_in, 16)
            sp.dma_start(proj[:, 0:F], wT).then_inc(consts_in, 16)
            sp.dma_start(edge_sb[:, :, :], edge.partition_broadcast(P)).then_inc(consts_in, 16)
            sp.dma_start(col_sb[:, :], edge_col).then_inc(consts_in, 16)
            sp.dma_start(fuse_sb[:, :, :], fuse).then_inc(consts_in, 16)
            sp.dma_start(rows_sb[:, :, :], rows.partition_broadcast(P)).then_inc(consts_in, 16)
            sp.dma_start(sel_sb[:, :], select).then_inc(consts_in, 16)
            sp.dma_start(ident_sb[:, :], ident).then_inc(consts_in, 16)
            sp.dma_start(pick_in, pick).then_inc(consts_in, 16)
            sp.dma_start(xT_all, xT).then_inc(xT_in, 16)
            with sp.Fori(0, STEPS // 2) as kk:
                for q in range(2):
                    sp.wait_ge(pos_ready, kk * 2 + q + 1)
                    sp.dma_start(adj_in[:, q, :], adjT[bass.ds(kk * 2 * P + q * P, P), :]).then_inc(adj_arrived[q], 16)
            sp.wait_ge(pos_ready, STEPS + 1)
            sp.dma_start(adj_in[:, 0, :], adjT[0:P, :]).then_inc(adj_arrived[0], 16)
            sp.wait_ge(agg_mm, AGG0 + NG * STEPS)
            sp.dma_start(x_all.rearrange("p (t f) -> p t f", f=F), x.rearrange("(t p) f -> p t f", p=P)).then_inc(x_in, 16)
            sp.wait_ge(agg_ready, 1 + NB * NG * NH)
            for g in range(NG):
                sp.dma_start(z_rows[g * HG:(g + 1) * HG, :], agg[D:P:HP, g, :]).then_inc(z_out, 16)
            sp.wait_ge(z_out, NG * 16)
            sp.dma_start(z_sb[:, :], z_rows.rearrange("h (a b) -> (h a) b", b=H * N // P)).then_inc(z_in, 16)
            sp.wait_ge(z_inv_ready, 1)
            sp.dma_start(z_inv_rows.rearrange("h (a b) -> (h a) b", b=H * N // P), z_sb[:, :]).then_inc(z_inv_out, 16)
            sp.wait_ge(z_inv_out, 16)
            for g in range(NG):
                sp.dma_start(agg[D:P:HP, g, :], z_inv_rows[g * HG:(g + 1) * HG, :]).then_inc(z_inv_in, 16)
            sp.wait_ge(y_ready, 1 + NC)
            with sp.Fori(0, STEPS // RING) as kk:
                for q in range(RING):
                    sp.wait_ge(e_ready, kk * RING + q + 1)
                    sp.dma_start(ring[:, q, :], adjT[bass.ds(kk * (RING * P) + q * P, P), :]).then_inc(ring_arrived[q], 16)
            sp.wait_ge(out_ready, 1)
            sp.dma_start(out.rearrange("(t p) f -> p t f", p=P), sq_all.rearrange("p (t f) -> p t f", f=F)).then_inc(stored, 16)
            sp.wait_ge(stored, 16)

        @block.gpsimd
        def _(pool):
            nc.gpsimd.memset(h_tile[:, :, :, :], 0.0).then_inc(zeroed, 1)
            nc.gpsimd.memset(src_cols[:, :], 0.0).then_inc(zeroed, 1)
            pool.wait_ge(zeroed, 2)
            nc.gpsimd.memset(h_tile[:, :, :, D:D + 1], 1.0).then_inc(zeroed, 1)
            nc.gpsimd.memset(q_rows[:, :].bitcast(F32), 0.0).then_inc(zeroed, 1)
            pool.wait_ge(xT_in, 16)
            with pool.Fori(0, NT // 2) as tt:
                for q in range(2):
                    pool.wait_ge(hid_mm, tt * 2 + q + 1)
                    nc.gpsimd.tensor_copy(xT_tile[:, q, :], xT_all[:, bass.ds(tt * 2 * P + q * P, P)]).then_inc(xT_tile_ready, 1)
            pool.wait_ge(d_max_ready, 1)
            nc.gpsimd.partition_all_reduce(d_top[:, :], d_max[:, :], P, RMAX).then_inc(d_top_ready, 1)
            pool.wait_ge(bad_ready[0], 1)
            nc.gpsimd.partition_all_reduce(in_range[:, 0, 1:2], in_range[:, 0, 0:1], P, RMAX).then_inc(any_bad_ready[0], 1)
            pool.wait_ge(score_max_ready, 1)
            nc.gpsimd.partition_all_reduce(score_top[:, 1:2], score_top[:, 0:1], P, RMAX).then_inc(score_top_ready, 1)
            pool.wait_ge(bad_ready[1], 1)
            nc.gpsimd.partition_all_reduce(in_range[:, 1, 1:2], in_range[:, 1, 0:1], P, RMAX).then_inc(any_bad_ready[1], 1)

        @block.tensor
        def _(pe):
            pe.sem_inc(hid_mm, 2)
            pe.sem_inc(agg_mm, AGG0)
            pe.sem_inc(z_mm, H)
            pe.sem_inc(y_mm, 1)
            pe.sem_inc(l1_mm, ES)
            pe.wait_ge(consts_in, CONSTS * 16)
            nc.tensor.matmul(ps[:, 0, 0:2 * H], w_sb[:, :], attn_sb[:, :], start=True, stop=True).then_inc(src_dst_mm, 1)
            pe.wait_ge(proj_ready, 3)
            with pe.Fori(0, NT // 2) as tt:
                for q in range(2):
                    pe.wait_ge(xT_tile_ready, tt * 2 + q + 1)
                    pe.wait_ge(hid_ready, tt * 2 + q + 1)
                    nc.tensor.matmul(ps[:, q, 0:F + H], xT_tile[:, q, :], proj[:, :], start=True, stop=True).then_inc(hid_mm, 1)
            for c in range(N // HALF):
                if c >= 4:
                    pe.wait_ge(q_scaled, c - 3)
                nc.tensor.matmul(ps[0:QR, 4 + c % 4, :], src_cols[:, :], xT_all[:, c * HALF:(c + 1) * HALF],
                                 start=True, stop=True).then_inc(q_mm, 1)
            sign = [pe.snap(nc.tensor.value_load(w_sign[0:1, h:h + 1], min_val=0, max_val=1) * IB) for h in range(H)]
            pe.wait_ge(hid_ready, NT + 2)
            pe.wait_ge(zeroed, 3)
            pe.wait_ge(q_ready, 3)
            pe.wait_ge(setup_ready, 1)
            with pe.Fori(0, NB) as ib:

                def sums(k, q, h):
                    s = h % 2
                    if h == 0:
                        pe.wait_ge(abs_ready, k + 1)
                        pe.wait_ge(lo_ready, k + 1)
                    pe.wait_ge(score_ready, k * H + h + 1)
                    for b in range(NH):
                        nc.tensor.matmul(z_ps[:, s, b, :], signed_id[:, h, :], hi[:, q, bass.ds(sign[h] + b * HALF, HALF)], start=True, stop=False)
                        nc.tensor.matmul(z_ps[:, s, b, :], signed_id[:, h, :], lo[:, q, b * HALF:(b + 1) * HALF], start=False, stop=False)
                    for b in range(NH):
                        last = nc.tensor.matmul(z_ps[:, s, b, :], pick_sb[:, h, :], q_rows[:, bass.ds(ib * IB + b * HALF, HALF)], start=False, stop=True)
                    last.then_inc(z_mm, 1)

                def gather(k, q, g, b, start, stop):
                    if b == 0:
                        pe.wait_ge(h_tile_ready, k + 1)
                        pe.wait_ge(weight_ready, k * H + (g + 1) * HG)
                    for c in range(HG):
                        last = nc.tensor.matmul(acc[c * HP:(c + 1) * HP, g, b, :], h_tile[:, q, g * HG + c, :],
                                                weights[:, q, g * HG + c, b * HALF:(b + 1) * HALF],
                                                start=start, stop=stop)
                    if b == NH - 1:
                        last.then_inc(agg_mm, 1)

                def step(k, q, start=False, stop=False, second=False):
                    for h in range(H):
                        sums(k, q, h)
                        if h == H // 2 and start:
                            pe.wait_ge(agg_ready, 1 + ib * (NG * NH))
                        if h % 2 and h < H // 2 and not start:
                            gather(k - 1, 1 - q, 1, h // 2, second, False)
                        if h % 2 and h > H // 2:
                            gather(k, q, 0, h // 2 - NH, start, stop)
                    if stop:
                        for b in range(NH):
                            gather(k, q, 1, b, False, True)

                step(ib * NT, 0, start=True)
                step(ib * NT + 1, 1, second=True)
                with pe.Fori(1, NT // 2 - 1) as jj:
                    for q in range(2):
                        step(ib * NT + jj * 2 + q, q)
                step(ib * NT + NT - 2, 0)
                step(ib * NT + NT - 1, 1, stop=True)

            def exact(n):
                with pe.Fori(0, NB * XH[n]) as u:
                    with pe.Fori(0, NT) as jt:
                        pe.wait_ge(x_weight_ready[n], u * NT + jt + 1)
                        if n == 0:
                            pe.wait_ge(x_h_ready, u * NT + jt + 1)
                            for b in range(NH):
                                last = nc.tensor.matmul(ps[0:HP, b, :], h_tile[:, 0, 0, :], logit_x[:, b * HALF:(b + 1) * HALF],
                                                        start=True, stop=True)
                        else:
                            for t in range(TB):
                                last = nc.tensor.matmul(ps[:, t, 0:F + 1], logit_x[:, t * P:(t + 1) * P],
                                                        fifth[:, bass.ds(jt * XW, F + 1)], start=True, stop=True)
                        last.then_inc(x_mm[n], 1)

            pe.wait_ge(any_bad_ready[0], 1)
            with nc.tensor.If(any_bad(nc.tensor, 0) > 0):
                exact(0)
            pe.wait_ge(z_inv_in, NG * 16)
            with pe.Fori(0, NC) as c:
                pe.wait_ge(agg_n_ready, c + 1)
                for g in range(NG):
                    last = nc.tensor.matmul(ps[:, g, :], sel_sb[:, :], agg[:, g, bass.ds(c * CH, CH)], start=True, stop=True)
                last.then_inc(spread_mm, 1)
                pe.wait_ge(agg_n_ready, c + 2)
                pe.wait_ge(y_ready, c + 1)
                for t in range(TC):
                    for g in range(NG):
                        last = nc.tensor.matmul(ps[:, 4, t * F:(t + 1) * F], agg_n[:, g, t * P:(t + 1) * P],
                                                fuse_sb[:, g, :], start=(g == 0), stop=(g == NG - 1))
                last.then_inc(y_mm, 1)
            pe.wait_ge(x1_ready, 1)
            with pe.Fori(0, NB) as ib:
                pe.wait_ge(l1_out, 1 + ib * TB)

                def step1(k, jt, q, start, stop):
                    pe.wait_ge(e_ready, RING + k + 1)
                    for t in range(TB):
                        last = nc.tensor.matmul(ps[:, t, 0:F + 1], e_all[:, q % ES, t * P:(t + 1) * P],
                                                fifth[:, bass.ds(jt * XW, F + 1)], start=start, stop=stop)
                    last.then_inc(l1_mm, 1)

                for q in range(ES):
                    step1(ib * NT + q, q, q, q == 0, False)
                with pe.Fori(1, NT // ES - 1) as jj:
                    for q in range(ES):
                        step1(ib * NT + jj * ES + q, jj * ES + q, q, False, False)
                for q in range(ES):
                    step1(ib * NT + NT - ES + q, NT - ES + q, q, False, q == ES - 1)
            pe.wait_ge(any_bad_ready[1], 1)
            with nc.tensor.If(any_bad(nc.tensor, 1) > 0):
                exact(1)

        @block.scalar
        def _(act):
            act.sem_inc(hid_ready, 2)
            act.sem_inc(agg_ready, 1)
            with act.Fori(0, NT // 2) as tt:
                for q in range(2):
                    act.wait_ge(hid_mm, 2 + tt * 2 + q + 1)
                    nc.scalar.copy(hid[:, bass.ds((tt * 2 + q) * F, F)], ps[:, q, 0:F]).then_inc(hid_copied, 1)
                    nc.scalar.copy(d_all[:, bass.ds((tt * 2 + q) * H, H)], ps[:, q, F:F + H]).then_inc(hid_copied, 1)
                    act.wait_ge(hid_copied, (tt * 2 + q + 1) * 2)
                    act.sem_inc(hid_ready, 1)
            act.wait_ge(heads_ready, 1)
            for c in range(N // HALF):
                act.wait_ge(q_mm, c + 1)
                nc.scalar.activation(q_all[:, c * HALF:(c + 1) * HALF], ps[0:QR, 4 + c % 4, :], ACT.Identity,
                                     scale=col_w[:, 1:2], bias=col_w[:, 2:3]).then_inc(q_scaled, 1)

            act.wait_ge(pos_ready, 3)
            act.wait_ge(setup_ready, 1)
            nc.scalar.copy(hi[:, 0, 0:IB], pos[:, :]).then_inc(hi_ready, 1)
            nc.scalar.activation(hi[:, 0, IB:2 * IB], pos[:, :], ACT.Abs).then_inc(abs_ready, 1)
            nc.scalar.mul(fifth_v[:, 0, 0:IB], pos[:, :], ALPHA).then_inc(fifth_ready, 1)
            act.wait_ge(zeroed, 3)
            with act.Fori(0, NB) as ib:
                with act.Fori(0, NT // 2) as jj:
                    for q in range(2):
                        k = ib * NT + jj * 2 + q
                        jt = jj * 2 + q
                        act.wait_ge(agg_mm, k * NG + NG)
                        nc.scalar.copy(h_tile[:, q, :, 0:D], hid[:, bass.ds(jt * F, F)].rearrange("p (h d) -> p h d", h=H)).then_inc(h_tile_ready, 1)
                        for h in range(H):
                            act.wait_ge(score_ready, SC0 + k * H + h + 1)
                            nc.scalar.activation(weights[:, q, h, :], weights[:, q, h, :], ACT.Exp,
                                                 scale=w_abs[:, h:h + 1], bias=exp_bias[:, bass.ds(jt * H + h, 1)]).then_inc(weight_ready, 1)
                            if h == 3:
                                act.wait_ge(pos_ready, k + 4)
                                act.wait_ge(z_mm, k * H + H)
                                nc.scalar.copy(hi[:, 1 - q, 0:IB], pos[:, :]).then_inc(hi_ready, 1)
                            if h == 4:
                                nc.scalar.activation(hi[:, 1 - q, IB:2 * IB], pos[:, :], ACT.Abs).then_inc(abs_ready, 1)
                            if h == 5:
                                nc.scalar.mul(fifth_v[:, 1 - q, 0:IB], pos[:, :], ALPHA).then_inc(fifth_ready, 1)
                act.wait_ge(agg_mm, AGG0 + ib * (NG * NT) + NG * NT)
                for g in range(NG):
                    for b in range(NH):
                        nc.scalar.copy(agg[:, g, bass.ds(ib * IB + b * HALF, HALF)], acc[:, g, b, :]).then_inc(agg_ready, 1)

            def exact(n):
                if n == 0:
                    act.sem_inc(x_sums_out, 16)
                    act.dma_start(q_dram, q_rows[0:QR, :].bitcast(F32)).then_inc(x_q_out, 16)
                    act.wait_ge(x_q_out, 16)
                with act.Fori(0, NB) as ib:
                    with act.Fori(0, XH[n]) as h:
                        u = ib * XH[n] + h
                        if n == 0:
                            act.dma_start(row_x, q_dram[bass.ds(h, 1), bass.ds(ib * IB, IB)].partition_broadcast(P)).then_inc(x_rows_in, 16)
                            act.dma_start(row_rest, q_dram[bass.ds(h + HP, 1), bass.ds(ib * IB, IB)].partition_broadcast(P)).then_inc(x_rows_in, 16)
                        with act.Fori(0, NT) as jt:
                            act.wait_ge(x_adj_used[n], u * (2 * NT) + jt + 1)
                            act.dma_start(adj_in[:, 0, :], adjT[bass.ds((ib * NT + jt) * P, P), :]).then_inc(x_adj_in[n], 16)
                        for f in range(FOLDS):
                            half = P >> (f + 1)
                            act.wait_ge(x_top_ready[n], u * (FOLDS + 1) + f + 1)
                            act.dma_start(fold_x[0:half, :], top_x[half:2 * half, :]).then_inc(x_half_in[n], 16)
                        act.wait_ge(x_top_ready[n], u * (FOLDS + 1) + FOLDS + 1)
                        act.dma_start(top_dram, top_x[0:1, :]).then_inc(x_top_out[n], 16)
                        act.wait_ge(x_top_out[n], u * 16 + 16)
                        act.dma_start(row_top, top_dram.partition_broadcast(P)).then_inc(x_row_top_in[n], 16)
                        with act.Fori(0, NT) as jt:
                            act.wait_ge(x_adj_used[n], u * (2 * NT) + NT + jt + 1)
                            act.dma_start(adj_in[:, 0, :], adjT[bass.ds((ib * NT + jt) * P, P), :]).then_inc(x_adj_in[n], 16)
                            if n == 0:
                                nc.scalar.copy(h_tile[:, 0, 0, 0:D], hid[:, bass.ds(jt * F + h * D, D)]).then_inc(x_h_ready, 1)
                            act.wait_ge(x_logit_ready[n], u * NT + jt + 1)
                            nc.scalar.activation(logit_x, logit_x, ACT.Exp).then_inc(x_exp_ready[n], 1)
                        if n == 0:
                            act.wait_ge(x_adj_used[n], u * (2 * NT) + 2 * NT + 1)
                            act.dma_start(sums_dram[bass.ds(h * HP, HP), bass.ds(ib * IB, IB)], acc_x[0]).then_inc(x_sums_out, 16)
                if n == 0:
                    act.wait_ge(x_sums_out, (NB * H + 1) * 16)
                    for g in range(NG):
                        act.dma_start(agg[:, g, :], sums_dram[g * P:(g + 1) * P, :]).then_inc(x_agg_in, 16)
                    act.wait_ge(x_agg_in, NG * 16)
                    for g in range(NG):
                        act.dma_start(z_rows[g * HG:(g + 1) * HG, :], agg[D:P:HP, g, :]).then_inc(x_z_out, 16)
                    act.wait_ge(x_z_out, NG * 16)
                    act.dma_start(z_sb[:, :], z_rows.rearrange("h (a b) -> (h a) b", b=H * N // P)).then_inc(x_z_in, 16)
                    act.wait_ge(x_z_in, 16)

            act.wait_ge(any_bad_ready[0], 1)
            with nc.scalar.If(any_bad(nc.scalar, 0) > 0):
                exact(0)
            for n in range(3):
                if n == 2:
                    act.wait_ge(score_top_ready, 1)
                    act.wait_ge(x1_ready, 1)
                    with act.Fori(0, NB) as ib:
                        with act.Fori(0, NT // RING) as jj:
                            for q in range(RING):
                                jt = jj * RING + q
                                k = ib * NT + jt
                                act.wait_ge(l1_mm, k + 1)
                                act.wait_ge(ring_arrived[q], ib * (16 * NT // RING) + jj * 16 + 16)
                                nc.scalar.activation(e_all[:, q % ES, :], ring[:, q, :], ACT.Exp,
                                                     scale=stat[:, 4, bass.ds(jt, 1)], bias=stat[:, 5, 0:1]).then_inc(e_raw, 1)
                    act.wait_ge(any_bad_ready[1], 1)
                    with nc.scalar.If(any_bad(nc.scalar, 1) > 0):
                        exact(1)
                act.wait_ge(var_ready, n + 1)
                nc.scalar.sqrt(stat[:, 3, :], stat[:, 2, :]).then_inc(std_ready, 1)

        @block.vector
        def _(dve):
            chain = [0]

            def tick(ins):
                chain[0] += 1
                return ins.then_inc(vec, 1)

            def link(ins):
                tick(ins)
                dve.wait_ge(vec, chain[0])

            dve.sem_inc(pos_ready, 2)
            dve.sem_inc(score_ready, SC0)
            dve.sem_inc(agg_n_ready, 1)
            dve.sem_inc(y_ready, 1)
            dve.sem_inc(e_ready, RING)
            dve.sem_inc(l1_out, 1)
            dve.wait_ge(consts_in, CONSTS * 16)
            dve.wait_ge(zeroed, 2)
            dve.wait_ge(src_dst_mm, 1)
            nc.vector.tensor_copy(proj[:, F:F + H], ps[:, 0, H:2 * H]).then_inc(proj_ready, 1)
            nc.vector.tensor_copy(src_cols[:, 0:H], ps[:, 0, 0:H]).then_inc(proj_ready, 1)
            nc.vector.tensor_copy(src_cols[:, HP:HP + H], ps[:, 0, 0:H]).then_inc(proj_ready, 1)
            tick(nc.vector.tensor_scalar(col_w[:, 0:1].bitcast(U32), col_sb[:, 0:1].bitcast(U32), 0x7FFFFFFF, None, ALU.bitwise_and))
            tick(nc.vector.tensor_scalar(w_abs[:, :].bitcast(U32), edge_sb[:, 0, :].bitcast(U32), 0x7FFFFFFF, None, ALU.bitwise_and))
            link(nc.vector.tensor_scalar(w_sign[:, :], edge_sb[:, 0, :].bitcast(U32), 31, None, ALU.logical_shift_right))
            tick(nc.vector.tensor_scalar(col_w[:, 0:1], col_w[:, 0:1], W_MIN, None, ALU.max))
            tick(nc.vector.tensor_scalar(w_abs[:, :], w_abs[:, :], W_MIN, None, ALU.max))
            link(nc.vector.tensor_copy(w_sgn[:, :], w_sign[:, :]))
            tick(nc.vector.reciprocal(col_w[:, 1:2], col_w[:, 0:1]))
            tick(nc.vector.reciprocal(w_inv[:, :], w_abs[:, :]))
            link(nc.vector.tensor_scalar(w_sgn[:, :], w_sgn[:, :], -2.0, 1.0, ALU.mult, ALU.add))
            link(nc.vector.tensor_scalar(col_w[:, 1:2], col_w[:, 1:2], 1.0 - ALPHA, None, ALU.mult))
            nc.vector.tensor_tensor(col_w[:, 2:3], col_sb[:, 1:2], col_w[:, 1:2], ALU.mult).then_inc(heads_ready, 1)
            for h in range(H):
                tick(nc.vector.tensor_scalar(signed_id[:, h, :], ident_sb[:, :], w_sgn[:, h:h + 1], None, ALU.mult))
            link(nc.vector.tensor_copy(pick_sb[:, :, :], pick_in))
            sign = [dve.snap(nc.vector.value_load(w_sign[0:1, h:h + 1], min_val=0, max_val=1) * IB) for h in range(H)]
            dve.wait_ge(q_scaled, N // HALF)
            dve.wait_ge(zeroed, 4)
            nc.vector.tensor_copy(q_rows[0:QR, :], q_all).then_inc(q_ready, 1)
            dve.wait_ge(q_ready, 1)
            nc.vector.tensor_tensor(q_rows[HP:QR, :], q_all[HP:QR, :], q_rows[HP:QR, :].bitcast(F32), ALU.subtract).then_inc(q_ready, 2)
            dve.wait_ge(hid_ready, NT + 2)
            nc.vector.tensor_reduce(d_max[:, :], d_all[:, :].rearrange("p (t h) -> p h t", h=H), AX.X, ALU.max).then_inc(d_max_ready, 1)
            d_v = d_all[:, :].rearrange("p (t h) -> p t h", h=H)
            tick(nc.vector.scalar_tensor_tensor(out=up_bias[:, :].rearrange("p (t h) -> p t h", h=H), in0=d_v, scalar=1.0 - ALPHA,
                                                in1=w_inv[:, :].unsqueeze(1).to_broadcast([P, NT, H]), op0=ALU.mult, op1=ALU.mult))
            dve.wait_ge(d_top_ready, 1)
            link(nc.vector.scalar_tensor_tensor(out=exp_bias[:, :].rearrange("p (t h) -> p t h", h=H), in0=d_v, scalar=ALPHA,
                                                in1=d_top[:, :].unsqueeze(1).to_broadcast([P, NT, H]), op0=ALU.mult, op1=ALU.subtract))
            dve.sem_inc(setup_ready, 1)

            def no_edges(k, q):
                nc.vector.tensor_scalar(pos[:, :], adj_in[:, q, :], 0.0, NO_EDGE, ALU.is_le, ALU.mult).then_inc(no_edge_ready, 1)

            def masked(k, q):
                dve.wait_ge(no_edge_ready, k + 1)
                nc.vector.tensor_tensor(pos[:, :], adj_in[:, q, :], pos[:, :], ALU.add).then_inc(pos_ready, 1)

            def rest(k, q):
                dve.wait_ge(hi_ready, k + 1)
                nc.vector.tensor_tensor(lo[:, q, :], pos[:, :], hi[:, q, 0:IB].bitcast(F32), ALU.subtract).then_inc(lo_ready, 1)

            def negative(k, q):
                dve.wait_ge(fifth_ready, k + 1)
                nc.vector.tensor_scalar(fifth_v[:, q, IB:2 * IB].bitcast(U32), fifth_v[:, q, 0:IB].bitcast(U32),
                                        0x80000000, None, ALU.bitwise_or).then_inc(fifth_neg_ready, 1)

            dve.wait_ge(adj_arrived[0], 16)
            no_edges(0, 0)
            masked(0, 0)
            rest(0, 0)
            negative(0, 0)
            with dve.Fori(0, NB) as ib:
                with dve.Fori(0, NT // 2) as jj:
                    for q in range(2):
                        jt = jj * 2 + q
                        k = ib * NT + jt
                        dve.wait_ge(fifth_neg_ready, k + 1)
                        for h in range(H):
                            if h % HG == 0:
                                dve.wait_ge(agg_mm, k * NG + h // HG + 1)
                            dve.wait_ge(z_mm, H + k * H + h + 1)
                            nc.vector.scalar_tensor_tensor(out=weights[:, q, h, :], in0=z_ps[:, h % 2, :, :].rearrange("p b n -> p (b n)"),
                                                           scalar=up_bias[:, bass.ds(jt * H + h, 1)],
                                                           in1=fifth_v[:, q, bass.ds(sign[h], IB)],
                                                           op0=ALU.add, op1=ALU.max).then_inc(score_ready, 1)
                            if h == 1:
                                dve.wait_ge(adj_arrived[1 - q], ib * (8 * NT) + jj * 16 + 16 * (1 + q))
                                dve.wait_ge(abs_ready, k + 1)
                                dve.wait_ge(lo_ready, k + 1)
                                no_edges(k + 1, 1 - q)
                            if h == 3:
                                masked(k + 1, 1 - q)
                            if h == 5:
                                rest(k + 1, 1 - q)
                            if h == 7:
                                negative(k + 1, 1 - q)

            def check(n, z, tmp):
                link(nc.vector.tensor_scalar(tmp, z, Z_LOW, None, ALU.is_ge))
                link(nc.vector.scalar_tensor_tensor(out=tmp, in0=z, scalar=Z_HIGH, in1=tmp, op0=ALU.is_le, op1=ALU.mult))
                link(nc.vector.tensor_reduce(in_range[:, n, 0:1], tmp, AX.X, ALU.min))
                nc.vector.tensor_scalar(in_range[:, n, 0:1], in_range[:, n, 0:1], -1.0, 1.0, ALU.mult, ALU.add).then_inc(bad_ready[n], 1)
                dve.wait_ge(any_bad_ready[n], 1)

            def exact(n):
                edge_op = (ALU.is_gt, ALU.not_equal)[n]
                no_edge_op = (ALU.is_le, ALU.is_equal)[n]
                fin = (0, TB + 3)[n]
                per_unit = (4 if n == 0 else 2) + NT * (6 if n == 0 else 4) + NT * (8 if n == 0 else 6) + fin
                dve.sem_inc(x_adj_used[n], 1)
                with dve.Fori(0, NB) as ib:
                    with dve.Fori(0, XH[n]) as h:
                        u = ib * XH[n] + h
                        count = [u * per_unit, 0]

                        def xtick(ins):
                            count[1] += 1
                            ins.then_inc(x_vec[n], 1)

                        def xsettle():
                            dve.wait_ge(x_vec[n], count[0] + count[1])

                        def xlink(ins):
                            xtick(ins)
                            xsettle()

                        def logits(jt):
                            if n == 0:
                                xlink(nc.vector.scalar_tensor_tensor(out=logit_x, in0=adj_in[:, 0, :], scalar=edge_sb[:, 0, bass.ds(h, 1)],
                                                                     in1=row_x, op0=ALU.mult, op1=ALU.add))
                                xlink(nc.vector.tensor_scalar(logit_x, logit_x, d_all[:, bass.ds(jt * H + h, 1)], None, ALU.add))
                                xlink(nc.vector.scalar_tensor_tensor(out=logit_x, in0=logit_x, scalar=ALPHA, in1=logit_x, op0=ALU.mult, op1=ALU.max))
                            else:
                                xlink(nc.vector.tensor_scalar(logit_x, adj_in[:, 0, :], stat[:, 4, bass.ds(jt, 1)], None, ALU.mult))
                            xlink(nc.vector.tensor_scalar(masked_x, adj_in[:, 0, :], 0.0, MASKED, no_edge_op, ALU.mult))
                            xlink(nc.vector.tensor_tensor(logit_x, logit_x, masked_x, ALU.add))

                        if n == 0:
                            dve.wait_ge(x_rows_in, u * 32 + 32)
                            xlink(nc.vector.tensor_tensor(row_x, row_x, row_rest, ALU.add))
                            xlink(nc.vector.tensor_scalar(row_x, row_x, w_abs[:, bass.ds(h, 1)], 1.0 / (1.0 - ALPHA), ALU.mult, ALU.mult))
                        xlink(nc.vector.memset(top_x, MASKED))
                        if n == 0:
                            dve.wait_ge(x_sums_out, u * 16 + 16)
                        xtick(nc.vector.memset(acc_x[n], 0.0))
                        head = count[1]
                        with dve.Fori(0, NT) as jt:
                            count[0], count[1] = u * per_unit + jt * (6 if n == 0 else 4), head
                            xsettle()
                            dve.wait_ge(x_adj_in[n], u * (32 * NT) + jt * 16 + 16)
                            logits(jt)
                            xlink(nc.vector.tensor_tensor(top_x, top_x, logit_x, ALU.max))
                            dve.sem_inc(x_adj_used[n], 1)
                        done = count[1] - head
                        assert done == (6 if n == 0 else 4)
                        dve.sem_inc(x_top_ready[n], 1)
                        for f in range(FOLDS):
                            half = P >> (f + 1)
                            dve.wait_ge(x_half_in[n], u * (16 * FOLDS) + f * 16 + 16)
                            nc.vector.tensor_tensor(top_x[0:half, :], top_x[0:half, :], fold_x[0:half, :], ALU.max).then_inc(x_top_ready[n], 1)
                            if f < FOLDS - 1:
                                dve.wait_ge(x_top_ready[n], u * (FOLDS + 1) + f + 2)
                        head += NT * done
                        with dve.Fori(0, NT) as jt:
                            count[0], count[1] = u * per_unit + jt * (8 if n == 0 else 6), head
                            dve.wait_ge(x_adj_in[n], u * (32 * NT) + 16 * NT + jt * 16 + 16)
                            dve.wait_ge(x_row_top_in[n], u * 16 + 16)
                            logits(jt)
                            xlink(nc.vector.tensor_tensor(logit_x, logit_x, row_top, ALU.subtract))
                            dve.sem_inc(x_logit_ready[n], 1)
                            dve.wait_ge(x_exp_ready[n], u * NT + jt + 1)
                            xlink(nc.vector.scalar_tensor_tensor(out=logit_x, in0=adj_in[:, 0, :], scalar=0.0, in1=logit_x, op0=edge_op, op1=ALU.mult))
                            dve.sem_inc(x_weight_ready[n], 1)
                            dve.wait_ge(x_mm[n], u * NT + jt + 1)
                            sums = ps[0:HP, 0:NH, :].rearrange("p b n -> p (b n)") if n == 0 else ps[:, :, 0:F + 1]
                            xlink(nc.vector.tensor_tensor(acc_x[n], acc_x[n], sums, ALU.add))
                            dve.sem_inc(x_adj_used[n], 1)
                        assert count[1] - head == (8 if n == 0 else 6)
                        count[0], count[1] = u * per_unit, head + NT * (count[1] - head)
                        if n == 1:
                            z1 = acc_x[1][:, :, F:F + 1].rearrange("p t o -> p (t o)")
                            xlink(nc.vector.tensor_scalar(z1_fix[:, :], z1, 0.0, None, ALU.is_equal))
                            xlink(nc.vector.tensor_tensor(z1_fix[:, :], z1_fix[:, :], z1, ALU.add))
                            xlink(nc.vector.reciprocal(z1_fix[:, :], z1_fix[:, :]))
                            for t in range(TB):
                                xtick(nc.vector.scalar_tensor_tensor(out=y_all[:, bass.ds(ib * IB + t * F, F)], in0=acc_x[1][:, t, 0:F],
                                                                     scalar=z1_fix[:, t:t + 1], in1=fifth[:, bass.ds(ib * (TB * XW) + t * XW, F)],
                                                                     op0=ALU.mult, op1=ALU.add))
                        assert count[1] == per_unit
                dve.wait_ge(x_vec[n], NB * XH[n] * per_unit)
                if n == 0:
                    dve.wait_ge(x_z_in, 16)

            dve.wait_ge(z_in, 16)
            check(0, z_sb[:, :], y_all[:, 0:H * N // P])
            with nc.vector.If(any_bad(nc.vector, 0) > 0):
                exact(0)
            nc.vector.reciprocal(z_sb[:, :], z_sb[:, :]).then_inc(z_inv_ready, 1)
            with dve.Fori(0, NC) as c:
                dve.wait_ge(spread_mm, c + 1)
                dve.wait_ge(y_mm, c + 1)
                nc.vector.tensor_tensor(agg_n[:, :, 0:CH], agg[:, :, bass.ds(c * CH, CH)], ps[:, 0:NG, :], ALU.mult).then_inc(agg_n_ready, 1)
                dve.wait_ge(y_mm, c + 2)
                nc.vector.tensor_tensor(y_all[:, bass.ds(c * CH, CH)].rearrange("p (t f) -> p t f", f=F),
                                        ps[:, 4, :].rearrange("p (t f) -> p t f", f=F),
                                        rows_sb[:, 0, :].unsqueeze(1).to_broadcast([P, TC, F]), ALU.add).then_inc(y_ready, 1)
            dve.wait_ge(y_ready, 1 + NC)

            def tiles(v):
                return v.rearrange("p (t f) -> p t f", f=F)

            def wide(v):
                return v.unsqueeze(2).to_broadcast([P, NT, F])

            def row(n):
                return rows_sb[:, n, :].unsqueeze(1).to_broadcast([P, NT, F])

            def normalise(dst, n):
                link(nc.vector.tensor_reduce(stat[:, 0, :], tiles(y_all), AX.X, ALU.add))
                link(nc.vector.tensor_scalar(stat[:, 0, :], stat[:, 0, :], 1.0 / F, None, ALU.mult))
                link(nc.vector.tensor_tensor(tiles(y_all), tiles(y_all), wide(stat[:, 0, :]), ALU.subtract))
                link(nc.vector.tensor_tensor(sq_all, y_all, y_all, ALU.mult))
                link(nc.vector.tensor_reduce(stat[:, 1, :], tiles(sq_all), AX.X, ALU.add))
                nc.vector.tensor_scalar(stat[:, 2, :], stat[:, 1, :], 1.0 / F, EPS, ALU.mult, ALU.add).then_inc(var_ready, 1)
                dve.wait_ge(std_ready, n)
                link(nc.vector.reciprocal(stat[:, 6, :], stat[:, 3, :]))
                return nc.vector.tensor_tensor(dst, tiles(y_all), wide(stat[:, 6, :]), ALU.mult)

            link(normalise(tiles(y_all), 1))
            link(nc.vector.tensor_tensor(tiles(y_all), tiles(y_all), row(1), ALU.mult))
            link(nc.vector.tensor_tensor(tiles(y_all), tiles(y_all), row(2), ALU.add))
            dve.wait_ge(x_in, 16)
            link(nc.vector.scalar_tensor_tensor(out=y_all, in0=y_all, scalar=0.0, in1=x_all, op0=ALU.max, op1=ALU.add))
            link(normalise(x1[:, :, 0:F], 2))
            link(nc.vector.memset(x1[:, :, F:F + 1], 1.0))
            link(nc.vector.tensor_tensor(tiles(sq_all), x1[:, :, 0:F], row(3), ALU.mult))
            link(nc.vector.tensor_reduce(stat[:, 4, :], tiles(sq_all), AX.X, ALU.add))
            nc.vector.tensor_reduce(score_top[:, 0:1], stat[:, 4, :], AX.X, ALU.max).then_inc(score_max_ready, 1)
            dve.wait_ge(score_top_ready, 1)
            nc.vector.tensor_scalar(stat[:, 5, 0:1], score_top[:, 1:2], 0.0, -1.0, ALU.max, ALU.mult).then_inc(x1_ready, 1)
            with dve.Fori(0, NB) as ib:
                with dve.Fori(0, NT // RING) as jj:
                    for q in range(RING):
                        k = ib * NT + jj * RING + q
                        dve.wait_ge(e_raw, k + 1)
                        nc.vector.scalar_tensor_tensor(out=e_all[:, q % ES, :], in0=ring[:, q, :], scalar=0.0, in1=e_all[:, q % ES, :],
                                                       op0=ALU.not_equal, op1=ALU.mult).then_inc(e_ready, 1)
                dve.wait_ge(l1_mm, ES + ib * NT + NT)
                z1 = ps[:, :, F:F + 1].rearrange("p t o -> p (t o)")
                nc.vector.tensor_copy(z1_all[:, bass.ds(ib * TB, TB)], z1).then_inc(l1_z, 1)
                nc.vector.tensor_scalar(z1_fix[:, :], z1, Z_LOW, None, ALU.is_lt).then_inc(l1_z, 1)
                dve.wait_ge(l1_z, ib * 4 + 2)
                nc.vector.tensor_tensor(z1_fix[:, :], z1_fix[:, :], z1, ALU.add).then_inc(l1_z, 1)
                dve.wait_ge(l1_z, ib * 4 + 3)
                nc.vector.reciprocal(z1_fix[:, :], z1_fix[:, :]).then_inc(l1_z, 1)
                dve.wait_ge(l1_z, ib * 4 + 4)
                for t in range(TB):
                    nc.vector.scalar_tensor_tensor(out=y_all[:, bass.ds(ib * IB + t * F, F)], in0=ps[:, t, 0:F], scalar=z1_fix[:, t:t + 1],
                                                   in1=fifth[:, bass.ds(ib * (TB * XW) + t * XW, F)], op0=ALU.mult, op1=ALU.add).then_inc(l1_out, 1)
            dve.wait_ge(l1_out, 1 + NB * TB)
            check(1, z1_all[:, :], sq_all[:, 0:NT])
            with nc.vector.If(any_bad(nc.vector, 1) > 0):
                exact(1)
            normalise(tiles(sq_all), 3).then_inc(out_ready, 1)


def kernel(x, adj, L0_gnn_W, L0_gnn_attn_src, L0_gnn_attn_dst, L0_gnn_edge_W, L0_gnn_edge_b, L0_gnn_fuse_W,
           L0_gnn_fuse_b, L0_gnn_ln_g, L0_gnn_ln_b, L1_gnn_H_v):
    import numpy as np
    import concourse.bacc as bacc
    from concourse import mybir as _mybir
    from concourse.bass_utils import run_bass_kernel_spmd

    x, adj, w, fuse_w = (np.asarray(a) for a in (x, adj, L0_gnn_W, L0_gnn_fuse_W))
    adj_t = adj.T.reshape(NT, P, NB, IB).transpose(2, 0, 1, 3).reshape(NB * NT * P, IB)
    attn = np.zeros((F, 2 * H), x.dtype)
    for h in range(H):
        attn[h * D:(h + 1) * D, h] = np.asarray(L0_gnn_attn_src)[h]
        attn[h * D:(h + 1) * D, H + h] = np.asarray(L0_gnn_attn_dst)[h]
    fuse = np.zeros((HG, HP, NG, F), x.dtype)
    fuse[:, 0:D] = fuse_w.T.reshape(NG, HG, D, F).transpose(1, 2, 0, 3)
    select = np.zeros((P, P), x.dtype)
    for c in range(HG):
        select[c * HP + D, c * HP:(c + 1) * HP] = 1.0
    rows = np.stack([np.asarray(a).reshape(F) for a in (L0_gnn_fuse_b, L0_gnn_ln_g, L0_gnn_ln_b, L1_gnn_H_v)])
    edge = np.stack([np.asarray(L0_gnn_edge_W).reshape(H), np.asarray(L0_gnn_edge_b).reshape(H)])
    edge_col = np.zeros((HP + H, 2), x.dtype)
    edge_col[0:H] = edge_col[HP:HP + H] = edge.T
    pick = np.zeros((P, H, P), x.dtype)
    for h in range(H):
        pick[h, h] = pick[HP + h, h] = 1.0
    arrays = {"xT": x.T, "x": x, "adjT": adj_t, "wT": w.T, "w": w, "attn": attn, "edge": edge, "edge_col": edge_col,
              "fuse": fuse.reshape(P, NG, F), "rows": rows, "select": select,
              "pick": pick, "ident": np.eye(P, dtype=x.dtype)}
    arrays = {n: np.ascontiguousarray(a) for n, a in arrays.items()}
    nc = bacc.Bacc("TRN2", target_bir_lowering=False, num_devices=1)
    args = [nc.dram_tensor(n, a.shape, _mybir.dt.from_np(a.dtype), kind="ExternalInput").ap() for n, a in arrays.items()]
    args.append(nc.dram_tensor("out", x.shape, _mybir.dt.from_np(x.dtype), kind="ExternalOutput").ap())
    gnn_kernel(nc, *args)
    return run_bass_kernel_spmd(nc, [arrays], core_ids=[0]).results[0]["out"]
```

```python
from contextlib import ExitStack

import concourse.bass as bass
from concourse import mybir

F32 = mybir.dt.float32
U32 = mybir.dt.uint32
F32R = mybir.dt.float32r
ALU = mybir.AluOpType
ACT = mybir.ActivationFunctionType
AX = mybir.AxisListType
RMAX = bass.bass_isa.ReduceOp.max

P = 128
N = 4096
F = 128
H = 8
D = F // H
HP = 32
HG = P // HP
NG = H // HG
NT = N // P
IB = 1024
NB = N // IB
HALF = 512
NH = IB // HALF
TB = IB // P
XW = 132
CH = 512
NC = N // CH
TC = CH // P
BS = TB // 2
BC = NC // NB
ALPHA = 0.2
EPS = 1e-5
NO_EDGE = -float(2.0 ** 100)
W_MIN = 1e-25
QR = HP + H
RING = 8
ES = 4
NX = 4
HT = 4
LNS = 4
CONSTS = 10
Z_LOW = 1e-25
Z_HIGH = 1e30
MASKED = -1e30
FOLDS = 7
AGG0 = 2 * NG
SC0 = 2


def gnn_kernel(nc, xT, x, adjT, wT, w, attn, edge, edge_col, fuse, rows, select, pick, ident, out):
    z_rows = nc.dram_tensor("z_rows", [H, N], F32, kind="Internal").ap()
    z_inv_rows = nc.dram_tensor("z_inv_rows", [H, N], F32, kind="Internal").ap()
    q_dram = nc.dram_tensor("q_dram", [QR, N], F32, kind="Internal").ap()
    sums_dram = nc.dram_tensor("sums_dram", [H * HP, N], F32, kind="Internal").ap()
    top_dram = nc.dram_tensor("top_dram", [1, IB], F32, kind="Internal").ap()
    with ExitStack() as ctx:
        def sb(name, shape, dt=F32):
            return ctx.enter_context(nc.sbuf_tensor(name, shape, dt))

        def sem(name):
            return ctx.enter_context(nc.semaphore(name))

        adj_in = sb("adj_in", [P, 2, IB])
        pos = sb("pos", [P, IB])
        hi = sb("hi", [P, 2, 2 * IB], F32R)
        lo = sb("lo", [P, 2, IB], F32R)
        fifth = sb("fifth", [P, NT * XW])
        fifth_v = fifth[:, 0:4 * IB].rearrange("p (q n) -> p q n", q=2)
        x1 = fifth[:, :].rearrange("p (t c) -> p t c", c=XW)
        big = sb("big", [P, 2 * H * IB])
        weights = big[:, :].rearrange("p (s h n) -> p s h n", s=2, h=H)
        xT_all = big[:, 0:N]
        pick_in = big[:, N:N + H * P].rearrange("p (h n) -> p h n", h=H)
        q_all = big[0:QR, 2 * N:3 * N]
        y_all = big[:, 0:N]
        sq_all = big[:, N:2 * N]
        x_all = big[:, 2 * N:3 * N]
        e_all = big[:, 3 * N:4 * N].rearrange("p (s n) -> p s n", s=4)
        q_rows = sb("q_rows", [P, N], F32R)
        hid = sb("hid", [P, NT * F])
        agg = sb("agg", [P, NG, N])
        ring = agg[:, :, :].rearrange("p g (s n) -> p (g s) n", n=IB)
        h_tile = sb("h_tile", [P, 2, H, HP])
        proj = sb("proj", [P, F + H])
        w_sb = sb("w_sb", [P, F])
        attn_sb = sb("attn_sb", [P, 2 * H])
        src_cols = sb("src_cols", [P, QR])
        edge_sb = sb("edge_sb", [P, 2, H])
        col_sb = sb("col_sb", [QR, 2])
        col_w = sb("col_w", [QR, 3])
        w_abs = sb("w_abs", [P, H])
        w_inv = sb("w_inv", [P, H])
        w_sign = sb("w_sign", [P, H], U32)
        w_sgn = sb("w_sgn", [P, H])
        signed_id = sb("signed_id", [P, H, P], F32R)
        pick_sb = sb("pick_sb", [P, H, P], F32R)
        ident_sb = sb("ident_sb", [P, P])
        d_all = sb("d_all", [P, NT * H])
        up_bias = sb("up_bias", [P, NT * H])
        exp_bias = sb("exp_bias", [P, NT * H])
        d_max = sb("d_max", [P, H])
        d_top = sb("d_top", [P, H])
        fuse_sb = sb("fuse_sb", [P, NG, F])
        rows_sb = sb("rows_sb", [P, 4, F])
        sel_sb = sb("sel_sb", [P, P])
        z_sb = sb("z_sb", [P, H * N // P])
        z_inv = sb("z_inv", [P, H * N // P])
        z1_fix = sb("z1_fix", [P, TB])
        agg_n = adj_in
        stat = sb("stat", [P, 6 + 3 * LNS, NT])
        eps_col = sb("eps_col", [P, 1])
        score_top = sb("score_top", [P, 2])
        z1_tmp = sb("z1_tmp", [P, NT])
        z1_all = sb("z1_all", [P, NT])
        zero_cols = sb("zero_cols", [P, 2 * XW])
        out_of_range = sb("out_of_range", [P, 2, 2])
        row_x = ring[:, 0, :]
        row_rest = ring[:, 1, :]
        top_x = ring[:, 2, :]
        logit_x = ring[:, 3, :]
        masked_x = ring[:, 4, :]
        fold_x = ring[:, 5, :]
        row_top = ring[:, 6, :]
        acc_x = (ring[0:HP, 7, :], sq_all[:, 0:TB * XW].rearrange("p (t c) -> p t c", c=XW)[:, :, 0:F + 1])

        ps = ctx.enter_context(nc.psum_tensor("ps", [P, 8, HALF], F32))
        acc = ps[:, 0:NG * NH, :].rearrange("p (g b) n -> p g b n", b=NH)
        z_ps = ps[:, NG * NH:8, :].rearrange("p (s b) n -> p s b n", b=NH)

        def sums1(s, t):
            return ps[:, s * BS + t // 2, t % 2 * XW:t % 2 * XW + F + 1]

        consts_in = sem("consts_in")
        xT_in = sem("xT_in")
        x_in = sem("x_in")
        adj_arrived = [sem(f"adj_arrived_{q}") for q in range(2)]
        src_dst_mm = sem("src_dst_mm")
        proj_ready = sem("proj_ready")
        hid_mm = sem("hid_mm")
        hid_ready = sem("hid_ready")
        d_ready = sem("d_ready")
        heads_ready = sem("heads_ready")
        q_mm = sem("q_mm")
        q_scaled = sem("q_scaled")
        q_ready = sem("q_ready")
        vec = sem("vec")
        d_max_ready = sem("d_max_ready")
        d_top_ready = sem("d_top_ready")
        setup_ready = sem("setup_ready")
        h_tile_ready = sem("h_tile_ready")
        no_edge_ready = sem("no_edge_ready")
        pos_ready = sem("pos_ready")
        hi_ready = sem("hi_ready")
        abs_ready = sem("abs_ready")
        lo_ready = sem("lo_ready")
        fifth_ready = sem("fifth_ready")
        fifth_neg_ready = sem("fifth_neg_ready")
        z_mm = sem("z_mm")
        score_ready = sem("score_ready")
        weight_ready = sem("weight_ready")
        agg_mm = sem("agg_mm")
        agg_ready = sem("agg_ready")
        zeroed = sem("zeroed")
        z_out = sem("z_out")
        z_in = sem("z_in")
        z_inv_ready = sem("z_inv_ready")
        z_inv_out = sem("z_inv_out")
        z_inv_in = sem("z_inv_in")
        spread_mm = sem("spread_mm")
        agg_n_ready = sem("agg_n_ready")
        y_mm = sem("y_mm")
        y_ready = sem("y_ready")
        mean_tick = [sem(f"mean_tick_{n}") for n in range(LNS)]
        res_tick = sem("res_tick")
        score_tick = sem("score_tick")
        mean_ready = [sem(f"mean_ready_{n}") for n in range(LNS)]
        squares_ready = [sem(f"squares_ready_{n}") for n in range(LNS)]
        deviation_ready = [sem(f"deviation_ready_{n}") for n in range(LNS)]
        scale_tick = [sem(f"scale_tick_{n}") for n in range(LNS)]
        prod_ready = sem("prod_ready")
        normed = [sem(f"normed_{n}") for n in range(LNS)]
        score_max_ready = sem("score_max_ready")
        score_top_ready = sem("score_top_ready")
        x1_ready = sem("x1_ready")
        ring_arrived = [sem(f"ring_arrived_{q}") for q in range(RING)]
        e_raw = sem("e_raw")
        e_ready = sem("e_ready")
        l1_mm = sem("l1_mm")
        l1_z = sem("l1_z")
        l1_out = sem("l1_out")
        stored = sem("stored")
        bad_ready = [sem(f"bad_ready_{n}") for n in range(2)]
        any_bad_ready = [sem(f"any_bad_ready_{n}") for n in range(2)]
        x_rows_in = sem("x_rows_in")
        x_q_out = sem("x_q_out")
        x_adj_in = [sem(f"x_adj_in_{n}") for n in range(2)]
        x_adj_used = [sem(f"x_adj_used_{n}") for n in range(2)]
        x_top_ready = [sem(f"x_top_ready_{n}") for n in range(2)]
        x_half_in = [sem(f"x_half_in_{n}") for n in range(2)]
        x_top_out = [sem(f"x_top_out_{n}") for n in range(2)]
        x_row_top_in = [sem(f"x_row_top_in_{n}") for n in range(2)]
        x_h_ready = sem("x_h_ready")
        x_logit_ready = [sem(f"x_logit_ready_{n}") for n in range(2)]
        x_exp_ready = [sem(f"x_exp_ready_{n}") for n in range(2)]
        x_weight_ready = [sem(f"x_weight_ready_{n}") for n in range(2)]
        x_mm = [sem(f"x_mm_{n}") for n in range(2)]
        x_sums_out = sem("x_sums_out")
        x_agg_in = sem("x_agg_in")
        x_z_out = sem("x_z_out")
        x_z_in = sem("x_z_in")
        x_z_inv_ready = sem("x_z_inv_ready")
        x_z_inv_out = sem("x_z_inv_out")
        x_z_inv_in = sem("x_z_inv_in")
        x_vec = [sem(f"x_vec_{n}") for n in range(2)]
        XH = (H, 1)

        def ln_stat(n, what, c, t=None):
            if t is None:
                return stat[:, 6 + 3 * n + what, bass.ds(c * TC, TC)]
            return stat[:, 6 + 3 * n + what, bass.ds(c * TC + t, 1)]

        def any_bad(engine, n):
            return engine.value_load(out_of_range[0:1, n, 1:2].bitcast(U32), min_val=0, max_val=0x3F800000)

        STEPS = NB * NT

        block = ctx.enter_context(nc.Block())

        @block.sync
        def _(sp):
            sp.dma_start(w_sb[:, :], w).then_inc(consts_in, 16)
            for c in range(NX):
                sp.dma_start(xT_all[:, c * (N // NX):(c + 1) * (N // NX)], xT[:, c * (N // NX):(c + 1) * (N // NX)]).then_inc(xT_in, 16)
            sp.dma_start(attn_sb[:, :], attn).then_inc(consts_in, 16)
            sp.dma_start(proj[:, 0:F], wT).then_inc(consts_in, 16)
            sp.dma_start(edge_sb[:, :, :], edge.partition_broadcast(P)).then_inc(consts_in, 16)
            sp.dma_start(col_sb[:, :], edge_col).then_inc(consts_in, 16)
            sp.dma_start(fuse_sb[:, :, :], fuse).then_inc(consts_in, 16)
            sp.dma_start(rows_sb[:, :, :], rows.partition_broadcast(P)).then_inc(consts_in, 16)
            sp.dma_start(sel_sb[:, :], select).then_inc(consts_in, 16)
            sp.dma_start(ident_sb[:, :], ident).then_inc(consts_in, 16)
            sp.dma_start(pick_in, pick).then_inc(consts_in, 16)
            with sp.Fori(0, STEPS // 2) as kk:
                for q in range(2):
                    sp.wait_ge(pos_ready, kk * 2 + q + 1)
                    sp.dma_start(adj_in[:, q, :], adjT[bass.ds(kk * 2 * P + q * P, P), :]).then_inc(adj_arrived[q], 16)
            sp.wait_ge(pos_ready, STEPS + 1)
            sp.dma_start(adj_in[:, 0, :], adjT[0:P, :]).then_inc(adj_arrived[0], 16)
            sp.wait_ge(agg_mm, AGG0 + NG * STEPS)
            sp.dma_start(x_all.rearrange("p (t f) -> p t f", f=F), x.rearrange("(t p) f -> p t f", p=P)).then_inc(x_in, 16)
            sp.wait_ge(agg_ready, NB * NG * NH)
            for g in range(NG):
                sp.dma_start(z_rows[g * HG:(g + 1) * HG, :], agg[D:P:HP, g, :]).then_inc(z_out, 16)
            sp.wait_ge(z_out, NG * 16)
            sp.dma_start(z_sb[:, :], z_rows.rearrange("h (a b) -> (h a) b", b=H * N // P)).then_inc(z_in, 16)
            sp.wait_ge(z_inv_ready, 1)
            sp.dma_start(z_inv_rows.rearrange("h (a b) -> (h a) b", b=H * N // P), z_inv[:, :]).then_inc(z_inv_out, 16)
            sp.wait_ge(z_inv_out, 16)
            for g in range(NG):
                sp.dma_start(agg[D:P:HP, g, :], z_inv_rows[g * HG:(g + 1) * HG, :]).then_inc(z_inv_in, 16)
            sp.wait_ge(y_ready, 1 + NC)
            with sp.Fori(0, STEPS // RING) as kk:
                for q in range(RING):
                    sp.wait_ge(e_ready, kk * RING + q + 1)
                    sp.dma_start(ring[:, q, :], adjT[bass.ds(kk * (RING * P) + q * P, P), :]).then_inc(ring_arrived[q], 16)

            def store(n):
                for c in range(NC):
                    sp.wait_ge(normed[n], (c + 1) * TC)
                    sp.dma_start(out[c * CH:(c + 1) * CH, :].rearrange("(t p) f -> p t f", p=P),
                                 y_all[:, c * CH:(c + 1) * CH].rearrange("p (t f) -> p t f", f=F)).then_inc(stored, 16)

            store(2)
            sp.wait_ge(stored, NC * 16)
            sp.wait_ge(any_bad_ready[1], 1)
            with nc.sync.If(any_bad(nc.sync, 1) > 0):
                store(3)
                sp.wait_ge(stored, 2 * NC * 16)

        @block.gpsimd
        def _(pool):
            nc.gpsimd.memset(h_tile[:, :, :, :], 0.0).then_inc(zeroed, 1)
            nc.gpsimd.memset(src_cols[:, :], 0.0).then_inc(zeroed, 1)
            pool.wait_ge(zeroed, 2)
            nc.gpsimd.memset(h_tile[:, :, :, D:D + 1], 1.0).then_inc(zeroed, 1)
            nc.gpsimd.memset(q_rows[:, :].bitcast(F32), 0.0).then_inc(zeroed, 1)
            nc.gpsimd.memset(zero_cols[:, :], 0.0).then_inc(zeroed, 1)
            pool.wait_ge(zeroed, 5)
            pool.wait_ge(q_ready, 1)
            nc.gpsimd.tensor_tensor(q_rows[HP:QR, :], q_all[HP:QR, :], q_rows[HP:QR, :].bitcast(F32), ALU.subtract).then_inc(q_ready, 2)
            pool.wait_ge(q_ready, 3)
            pool.wait_ge(d_max_ready, 1)
            nc.gpsimd.partition_all_reduce(d_top[:, :], d_max[:, :], P, RMAX).then_inc(d_top_ready, 1)
            pool.wait_ge(bad_ready[0], 1)
            nc.gpsimd.partition_all_reduce(out_of_range[:, 0, 1:2], out_of_range[:, 0, 0:1], P, RMAX).then_inc(any_bad_ready[0], 1)
            with pool.Fori(0, NC) as c:
                pool.wait_ge(normed[1], c * TC + TC)
                x1_c = fifth[:, bass.ds(c * (TC * XW), TC * XW)].rearrange("p (t c) -> p t c", c=XW)[:, :, 0:F]
                nc.gpsimd.tensor_tensor(sq_all[:, bass.ds(c * CH, CH)].rearrange("p (t f) -> p t f", f=F), x1_c,
                                        rows_sb[:, 3, :].unsqueeze(1).to_broadcast([P, TC, F]), ALU.mult).then_inc(prod_ready, 1)
            pool.wait_ge(prod_ready, NC)
            pool.wait_ge(score_max_ready, 1)
            nc.gpsimd.partition_all_reduce(score_top[:, 1:2], score_top[:, 0:1], P, RMAX).then_inc(score_top_ready, 1)
            pool.wait_ge(bad_ready[1], 1)
            nc.gpsimd.partition_all_reduce(out_of_range[:, 1, 1:2], out_of_range[:, 1, 0:1], P, RMAX).then_inc(any_bad_ready[1], 1)

        @block.tensor
        def _(pe):
            pe.sem_inc(agg_mm, AGG0)
            pe.sem_inc(z_mm, H)
            pe.sem_inc(y_mm, 1)
            pe.sem_inc(l1_mm, ES)
            pe.wait_ge(consts_in, CONSTS * 16)
            nc.tensor.matmul(ps[:, 0, 0:2 * H], w_sb[:, :], attn_sb[:, :], start=True, stop=True).then_inc(src_dst_mm, 1)
            pe.wait_ge(proj_ready, 3)
            pe.wait_ge(xT_in, NX * 16)
            for c in range(N // HALF):
                if c >= 4:
                    pe.wait_ge(q_scaled, c - 3)
                nc.tensor.matmul(ps[0:QR, 4 + c % 4, :], src_cols[:, :], xT_all[:, c * HALF:(c + 1) * HALF],
                                 start=True, stop=True).then_inc(q_mm, 1)
            pe.wait_ge(heads_ready, 1)
            sign = [pe.snap(nc.tensor.value_load(w_sign[0:1, h:h + 1], min_val=0, max_val=1) * IB) for h in range(H)]
            for i in range(NT // HT):
                if i == 1:
                    pe.wait_ge(q_scaled, N // HALF)
                if i >= 2:
                    pe.wait_ge(hid_ready, i - 1)
                for t in range(HT):
                    last = nc.tensor.matmul(ps[:, i % 2 * HT + t, 0:F + H], xT_all[:, (i * HT + t) * P:(i * HT + t + 1) * P], proj[:, :],
                                            start=True, stop=True)
                last.then_inc(hid_mm, 1)
            pe.wait_ge(hid_ready, NT // HT)
            pe.wait_ge(d_ready, NT // HT)
            pe.wait_ge(zeroed, 3)
            pe.wait_ge(q_ready, 3)
            pe.wait_ge(setup_ready, 1)
            def sums(ib, k, q, h):
                s = h % 2
                if h == 0:
                    pe.wait_ge(abs_ready, k + 1)
                    pe.wait_ge(lo_ready, k + 1)
                pe.wait_ge(score_ready, k * H + h + 1)
                for b in range(NH):
                    nc.tensor.matmul(z_ps[:, s, b, :], signed_id[:, h, :], hi[:, q, bass.ds(sign[h] + b * HALF, HALF)], start=True, stop=False)
                    nc.tensor.matmul(z_ps[:, s, b, :], signed_id[:, h, :], lo[:, q, b * HALF:(b + 1) * HALF], start=False, stop=False)
                for b in range(NH):
                    last = nc.tensor.matmul(z_ps[:, s, b, :], pick_sb[:, h, :], q_rows[:, bass.ds(ib * IB + b * HALF, HALF)], start=False, stop=True)
                last.then_inc(z_mm, 1)

            def gather(k, q, g, b, start, stop):
                if b == 0:
                    pe.wait_ge(h_tile_ready, k + 1)
                    pe.wait_ge(weight_ready, k * H + (g + 1) * HG)
                for c in range(HG):
                    last = nc.tensor.matmul(acc[c * HP:(c + 1) * HP, g, b, :], h_tile[:, q, g * HG + c, :],
                                            weights[:, q, g * HG + c, b * HALF:(b + 1) * HALF],
                                            start=start, stop=stop)
                if b == NH - 1:
                    last.then_inc(agg_mm, 1)

            def block_sums(ib, previous):

                def step(k, q, start=False, second=False, stop=False):
                    for h in range(H):
                        sums(ib, k, q, h)
                        if h == 1 and second and previous:
                            pe.wait_ge(agg_ready, ib * (NG * NH))
                        if h % 2 and h < H // 2 and (previous or not start):
                            gather(k - 1, 1 - q, 1, h // 2, second, start)
                        if h == H // 2 and start and previous:
                            pe.wait_ge(agg_ready, ib * (NG * NH) - NH)
                        if h % 2 and h > H // 2:
                            gather(k, q, 0, h // 2 - NH, start, stop)

                step(ib * NT, 0, start=True)
                step(ib * NT + 1, 1, second=True)
                with pe.Fori(1, NT // 2 - 1) as jj:
                    for q in range(2):
                        step(ib * NT + jj * 2 + q, q)
                step(ib * NT + NT - 2, 0)
                step(ib * NT + NT - 1, 1, stop=True)

            block_sums(0, False)
            with pe.Fori(1, NB) as ib:
                block_sums(ib, True)
            for b in range(NH):
                gather(STEPS - 1, 1, 1, b, False, True)

            def exact(n):
                with pe.Fori(0, NB * XH[n]) as u:
                    with pe.Fori(0, NT) as jt:
                        pe.wait_ge(x_weight_ready[n], u * NT + jt + 1)
                        if n == 0:
                            pe.wait_ge(x_h_ready, u * NT + jt + 1)
                            for b in range(NH):
                                last = nc.tensor.matmul(ps[0:HP, b, :], h_tile[:, 0, 0, :], logit_x[:, b * HALF:(b + 1) * HALF],
                                                        start=True, stop=True)
                        else:
                            for t in range(TB):
                                last = nc.tensor.matmul(ps[:, t, 0:F + 1], logit_x[:, t * P:(t + 1) * P],
                                                        fifth[:, bass.ds(jt * XW, F + 1)], start=True, stop=True)
                        last.then_inc(x_mm[n], 1)

            pe.wait_ge(any_bad_ready[0], 1)
            with nc.tensor.If(any_bad(nc.tensor, 0) > 0):
                exact(0)
                pe.wait_ge(x_z_inv_in, NG * 16)
            pe.wait_ge(z_inv_in, NG * 16)
            with pe.Fori(0, NC) as c:
                pe.wait_ge(agg_n_ready, c + 1)
                for g in range(NG):
                    last = nc.tensor.matmul(ps[:, g, :], sel_sb[:, :], agg[:, g, bass.ds(c * CH, CH)], start=True, stop=True)
                last.then_inc(spread_mm, 1)
                pe.wait_ge(agg_n_ready, c + 2)
                pe.wait_ge(y_ready, c + 1)
                for t in range(TC):
                    for g in range(NG):
                        last = nc.tensor.matmul(ps[:, 4, t * F:(t + 1) * F], agg_n[:, g, t * P:(t + 1) * P],
                                                fuse_sb[:, g, :], start=(g == 0), stop=(g == NG - 1))
                last.then_inc(y_mm, 1)
            pe.wait_ge(x1_ready, 1)
            pe.wait_ge(zeroed, 5)
            with pe.Fori(0, NB // 2) as pair:
                for s in range(2):
                    ib = pair * 2 + s
                    pe.wait_ge(l1_out, 1 + ib * TB)

                    for b in range(BS):
                        nc.tensor.matmul(ps[:, s * BS + b, 0:2 * XW], ident_sb[:, :], zero_cols[:, :], start=True, stop=False)

                    def step1(k, jt, q, stop):
                        pe.wait_ge(e_ready, RING + k + 1)
                        for t in range(TB):
                            last = nc.tensor.matmul(sums1(s, t), e_all[:, q % ES, t * P:(t + 1) * P],
                                                    fifth[:, bass.ds(jt * XW, F + 1)], start=False, stop=stop and t % 2 == 1)
                        last.then_inc(l1_mm, 1)

                    for q in range(ES):
                        step1(ib * NT + q, q, q, False)
                    with pe.Fori(1, NT // ES - 1) as jj:
                        for q in range(ES):
                            step1(ib * NT + jj * ES + q, jj * ES + q, q, False)
                    for q in range(ES):
                        step1(ib * NT + NT - ES + q, NT - ES + q, q, q == ES - 1)
            pe.wait_ge(any_bad_ready[1], 1)
            with nc.tensor.If(any_bad(nc.tensor, 1) > 0):
                exact(1)

        @block.scalar
        def _(act):
            act.wait_ge(heads_ready, 1)
            for c in range(N // HALF):
                act.wait_ge(q_mm, c + 1)
                nc.scalar.activation(q_all[:, c * HALF:(c + 1) * HALF], ps[0:QR, 4 + c % 4, :], ACT.Identity,
                                     scale=col_w[:, 1:2], bias=col_w[:, 2:3]).then_inc(q_scaled, 1)
            act.wait_ge(pos_ready, 3)
            nc.scalar.copy(hi[:, 0, 0:IB], pos[:, :]).then_inc(hi_ready, 1)
            nc.scalar.activation(hi[:, 0, IB:2 * IB], pos[:, :], ACT.Abs).then_inc(abs_ready, 1)
            nc.scalar.mul(fifth_v[:, 0, 0:IB], pos[:, :], ALPHA).then_inc(fifth_ready, 1)
            for i in range(NT // HT):
                act.wait_ge(hid_mm, i + 1)
                act.wait_ge(d_ready, i + 1)
                nc.scalar.copy(hid[:, i * HT * F:(i + 1) * HT * F].rearrange("p (t f) -> p t f", f=F),
                               ps[:, i % 2 * HT:(i % 2 + 1) * HT, 0:F]).then_inc(hid_ready, 1)
            act.wait_ge(hid_ready, NT // HT)
            act.wait_ge(setup_ready, 1)
            act.wait_ge(zeroed, 3)

            def leave(ib, g):
                act.wait_ge(agg_mm, AGG0 + ib * (NG * NT) + NG * NT - NG + g + 1)
                for b in range(NH):
                    nc.scalar.copy(agg[:, g, bass.ds(ib * IB + b * HALF, HALF)], acc[:, g, b, :]).then_inc(agg_ready, 1)

            def step(ib, jt, q, previous=False):
                k = ib * NT + jt
                if previous:
                    leave(ib - 1, 0)
                act.wait_ge(agg_mm, k * NG + NG)
                nc.scalar.copy(h_tile[:, q, :, 0:D], hid[:, bass.ds(jt * F, F)].rearrange("p (h d) -> p h d", h=H)).then_inc(h_tile_ready, 1)
                for h in range(H):
                    act.wait_ge(score_ready, SC0 + k * H + h + 1)
                    nc.scalar.activation(weights[:, q, h, :], weights[:, q, h, :], ACT.Exp,
                                         scale=w_abs[:, h:h + 1], bias=exp_bias[:, bass.ds(jt * H + h, 1)]).then_inc(weight_ready, 1)
                    if h == 3:
                        act.wait_ge(pos_ready, k + 4)
                        act.wait_ge(z_mm, k * H + H)
                        nc.scalar.copy(hi[:, 1 - q, 0:IB], pos[:, :]).then_inc(hi_ready, 1)
                    if h == 4:
                        nc.scalar.activation(hi[:, 1 - q, IB:2 * IB], pos[:, :], ACT.Abs).then_inc(abs_ready, 1)
                    if h == 5:
                        nc.scalar.mul(fifth_v[:, 1 - q, 0:IB], pos[:, :], ALPHA).then_inc(fifth_ready, 1)
                if previous:
                    leave(ib - 1, 1)

            def block_weights(ib, previous):
                step(ib, 0, 0, previous)
                step(ib, 1, 1)
                with act.Fori(1, NT // 2) as jj:
                    for q in range(2):
                        step(ib, jj * 2 + q, q)

            block_weights(0, False)
            with act.Fori(1, NB) as ib:
                block_weights(ib, True)
            for g in range(NG):
                leave(NB - 1, g)

            def exact(n):
                if n == 0:
                    act.sem_inc(x_sums_out, 16)
                    act.dma_start(q_dram, q_rows[0:QR, :].bitcast(F32)).then_inc(x_q_out, 16)
                    act.wait_ge(x_q_out, 16)
                with act.Fori(0, NB) as ib:
                    with act.Fori(0, XH[n]) as h:
                        u = ib * XH[n] + h
                        if n == 0:
                            act.dma_start(row_x, q_dram[bass.ds(h, 1), bass.ds(ib * IB, IB)].partition_broadcast(P)).then_inc(x_rows_in, 16)
                            act.dma_start(row_rest, q_dram[bass.ds(h + HP, 1), bass.ds(ib * IB, IB)].partition_broadcast(P)).then_inc(x_rows_in, 16)
                        with act.Fori(0, NT) as jt:
                            act.wait_ge(x_adj_used[n], u * (2 * NT) + jt + 1)
                            act.dma_start(adj_in[:, 0, :], adjT[bass.ds((ib * NT + jt) * P, P), :]).then_inc(x_adj_in[n], 16)
                        for f in range(FOLDS):
                            half = P >> (f + 1)
                            act.wait_ge(x_top_ready[n], u * (FOLDS + 1) + f + 1)
                            act.dma_start(fold_x[0:half, :], top_x[half:2 * half, :]).then_inc(x_half_in[n], 16)
                        act.wait_ge(x_top_ready[n], u * (FOLDS + 1) + FOLDS + 1)
                        act.dma_start(top_dram, top_x[0:1, :]).then_inc(x_top_out[n], 16)
                        act.wait_ge(x_top_out[n], u * 16 + 16)
                        act.dma_start(row_top, top_dram.partition_broadcast(P)).then_inc(x_row_top_in[n], 16)
                        with act.Fori(0, NT) as jt:
                            act.wait_ge(x_adj_used[n], u * (2 * NT) + NT + jt + 1)
                            act.dma_start(adj_in[:, 0, :], adjT[bass.ds((ib * NT + jt) * P, P), :]).then_inc(x_adj_in[n], 16)
                            if n == 0:
                                nc.scalar.copy(h_tile[:, 0, 0, 0:D], hid[:, bass.ds(jt * F + h * D, D)]).then_inc(x_h_ready, 1)
                            act.wait_ge(x_logit_ready[n], u * NT + jt + 1)
                            nc.scalar.activation(logit_x, logit_x, ACT.Exp).then_inc(x_exp_ready[n], 1)
                        if n == 0:
                            act.wait_ge(x_adj_used[n], u * (2 * NT) + 2 * NT + 1)
                            act.dma_start(sums_dram[bass.ds(h * HP, HP), bass.ds(ib * IB, IB)], acc_x[0]).then_inc(x_sums_out, 16)
                if n == 0:
                    act.wait_ge(x_sums_out, (NB * H + 1) * 16)
                    for g in range(NG):
                        act.dma_start(agg[:, g, :], sums_dram[g * P:(g + 1) * P, :]).then_inc(x_agg_in, 16)
                    act.wait_ge(x_agg_in, NG * 16)
                    for g in range(NG):
                        act.dma_start(z_rows[g * HG:(g + 1) * HG, :], agg[D:P:HP, g, :]).then_inc(x_z_out, 16)
                    act.wait_ge(x_z_out, NG * 16)
                    act.dma_start(z_sb[:, :], z_rows.rearrange("h (a b) -> (h a) b", b=H * N // P)).then_inc(x_z_in, 16)
                    act.wait_ge(x_z_inv_ready, 1)
                    act.dma_start(z_inv_rows.rearrange("h (a b) -> (h a) b", b=H * N // P), z_inv[:, :]).then_inc(x_z_inv_out, 16)
                    act.wait_ge(x_z_inv_out, 16)
                    for g in range(NG):
                        act.dma_start(agg[D:P:HP, g, :], z_inv_rows[g * HG:(g + 1) * HG, :]).then_inc(x_z_inv_in, 16)

            act.wait_ge(any_bad_ready[0], 1)
            with nc.scalar.If(any_bad(nc.scalar, 0) > 0):
                act.wait_ge(z_inv_in, NG * 16)
                exact(0)

            def squares(n, c):
                act.wait_ge(mean_ready[n], c + 1)
                for t in range(TC):
                    col = bass.ds(c * CH + t * F, F)
                    last = nc.scalar.activation(sq_all[:, col], y_all[:, col], ACT.Square, bias=ln_stat(n, 0, c, t),
                                                accum_out=ln_stat(n, 1, c, t))
                last.then_inc(squares_ready[n], 1)
                act.wait_ge(squares_ready[n], c + 1)
                nc.scalar.activation(ln_stat(n, 2, c), ln_stat(n, 1, c), ACT.Sqrt, scale=1.0 / F, bias=eps_col[:, :]).then_inc(deviation_ready[n], 1)

            squares(0, 0)
            with act.Fori(1, NC) as i:
                squares(1, i - 1)
                squares(0, i)
            squares(1, NC - 1)
            act.wait_ge(score_top_ready, 1)
            act.wait_ge(x1_ready, 1)

            def exps(ib, jj):
                for q in range(RING):
                    jt = jj * RING + q
                    k = ib * NT + jt
                    act.wait_ge(l1_mm, k + 1)
                    act.wait_ge(ring_arrived[q], ib * (16 * NT // RING) + jj * 16 + 16)
                    nc.scalar.activation(e_all[:, q % ES, :], ring[:, q, :], ACT.Exp,
                                         scale=stat[:, 4, bass.ds(jt, 1)], bias=stat[:, 5, 0:1]).then_inc(e_raw, 1)

            with act.Fori(0, NT // RING) as jj:
                exps(0, jj)
            with act.Fori(1, NB) as ib:
                exps(ib, 0)
                exps(ib, 1)
                for n in range(BC):
                    squares(2, ib * BC - BC + n)
                with act.Fori(2, NT // RING) as jj:
                    exps(ib, jj)
            for c in range(NC - BC, NC):
                squares(2, c)
            act.wait_ge(any_bad_ready[1], 1)
            with nc.scalar.If(any_bad(nc.scalar, 1) > 0):
                exact(1)
                with act.Fori(0, NC) as c:
                    squares(3, c)


        @block.vector
        def _(dve):
            chain = [0]

            def tick(ins):
                chain[0] += 1
                return ins.then_inc(vec, 1)

            def link(ins):
                tick(ins)
                dve.wait_ge(vec, chain[0])

            dve.sem_inc(pos_ready, 2)
            dve.sem_inc(score_ready, SC0)
            dve.sem_inc(agg_n_ready, 1)
            dve.sem_inc(y_ready, 1)
            dve.sem_inc(e_ready, RING)
            dve.sem_inc(l1_out, 1 + TB)
            def no_edges(k, q):
                nc.vector.tensor_scalar(pos[:, :], adj_in[:, q, :], 0.0, NO_EDGE, ALU.is_le, ALU.mult).then_inc(no_edge_ready, 1)

            def masked(k, q):
                dve.wait_ge(no_edge_ready, k + 1)
                nc.vector.tensor_tensor(pos[:, :], adj_in[:, q, :], pos[:, :], ALU.add).then_inc(pos_ready, 1)

            def rest(k, q):
                dve.wait_ge(hi_ready, k + 1)
                nc.vector.tensor_tensor(lo[:, q, :], pos[:, :], hi[:, q, 0:IB].bitcast(F32), ALU.subtract).then_inc(lo_ready, 1)

            def negative(k, q):
                dve.wait_ge(fifth_ready, k + 1)
                nc.vector.tensor_scalar(fifth_v[:, q, IB:2 * IB].bitcast(U32), fifth_v[:, q, 0:IB].bitcast(U32),
                                        0x80000000, None, ALU.bitwise_or).then_inc(fifth_neg_ready, 1)

            dve.wait_ge(consts_in, CONSTS * 16)
            dve.wait_ge(zeroed, 2)
            dve.wait_ge(src_dst_mm, 1)
            nc.vector.tensor_copy(proj[:, F:F + H], ps[:, 0, H:2 * H]).then_inc(proj_ready, 1)
            nc.vector.tensor_copy(src_cols[:, 0:H], ps[:, 0, 0:H]).then_inc(proj_ready, 1)
            nc.vector.tensor_copy(src_cols[:, HP:HP + H], ps[:, 0, 0:H]).then_inc(proj_ready, 1)
            tick(nc.vector.tensor_scalar(col_w[:, 0:1].bitcast(U32), col_sb[:, 0:1].bitcast(U32), 0x7FFFFFFF, None, ALU.bitwise_and))
            tick(nc.vector.tensor_scalar(w_abs[:, :].bitcast(U32), edge_sb[:, 0, :].bitcast(U32), 0x7FFFFFFF, None, ALU.bitwise_and))
            link(nc.vector.tensor_scalar(w_sign[:, :], edge_sb[:, 0, :].bitcast(U32), 31, None, ALU.logical_shift_right))
            tick(nc.vector.tensor_scalar(col_w[:, 0:1], col_w[:, 0:1], W_MIN, None, ALU.max))
            tick(nc.vector.tensor_scalar(w_abs[:, :], w_abs[:, :], W_MIN, None, ALU.max))
            link(nc.vector.tensor_copy(w_sgn[:, :], w_sign[:, :]))
            tick(nc.vector.reciprocal(col_w[:, 1:2], col_w[:, 0:1]))
            tick(nc.vector.reciprocal(w_inv[:, :], w_abs[:, :]))
            link(nc.vector.tensor_scalar(w_sgn[:, :], w_sgn[:, :], -2.0, 1.0, ALU.mult, ALU.add))
            link(nc.vector.tensor_scalar(col_w[:, 1:2], col_w[:, 1:2], 1.0 - ALPHA, None, ALU.mult))
            nc.vector.tensor_tensor(col_w[:, 2:3], col_sb[:, 1:2], col_w[:, 1:2], ALU.mult).then_inc(heads_ready, 1)
            for h in range(H):
                tick(nc.vector.tensor_scalar(signed_id[:, h, :], ident_sb[:, :], w_sgn[:, h:h + 1], None, ALU.mult))
            link(nc.vector.tensor_copy(pick_sb[:, :, :], pick_in))
            dve.wait_ge(adj_arrived[0], 16)
            no_edges(0, 0)
            masked(0, 0)
            sign = [dve.snap(nc.vector.value_load(w_sign[0:1, h:h + 1], min_val=0, max_val=1) * IB) for h in range(H)]
            dve.wait_ge(q_scaled, N // HALF)
            dve.wait_ge(zeroed, 4)
            nc.vector.tensor_copy(q_rows[0:QR, :], q_all).then_inc(q_ready, 1)
            rest(0, 0)
            negative(0, 0)
            for i in range(NT // HT):
                dve.wait_ge(hid_mm, i + 1)
                nc.vector.tensor_copy(d_all[:, i * HT * H:(i + 1) * HT * H].rearrange("p (t h) -> p t h", h=H),
                                      ps[:, i % 2 * HT:(i % 2 + 1) * HT, F:F + H]).then_inc(d_ready, 1)
            dve.wait_ge(d_ready, NT // HT)
            nc.vector.tensor_reduce(d_max[:, :], d_all[:, :].rearrange("p (t h) -> p h t", h=H), AX.X, ALU.max).then_inc(d_max_ready, 1)
            d_v = d_all[:, :].rearrange("p (t h) -> p t h", h=H)
            tick(nc.vector.scalar_tensor_tensor(out=up_bias[:, :].rearrange("p (t h) -> p t h", h=H), in0=d_v, scalar=1.0 - ALPHA,
                                                in1=w_inv[:, :].unsqueeze(1).to_broadcast([P, NT, H]), op0=ALU.mult, op1=ALU.mult))
            dve.wait_ge(d_top_ready, 1)
            link(nc.vector.scalar_tensor_tensor(out=exp_bias[:, :].rearrange("p (t h) -> p t h", h=H), in0=d_v, scalar=ALPHA,
                                                in1=d_top[:, :].unsqueeze(1).to_broadcast([P, NT, H]), op0=ALU.mult, op1=ALU.subtract))
            dve.sem_inc(setup_ready, 1)

            with dve.Fori(0, NB) as ib:
                with dve.Fori(0, NT // 2) as jj:
                    for q in range(2):
                        jt = jj * 2 + q
                        k = ib * NT + jt
                        dve.wait_ge(fifth_neg_ready, k + 1)
                        for h in range(H):
                            if h % HG == 0:
                                dve.wait_ge(agg_mm, k * NG + h // HG + 1)
                            dve.wait_ge(z_mm, H + k * H + h + 1)
                            nc.vector.scalar_tensor_tensor(out=weights[:, q, h, :], in0=z_ps[:, h % 2, :, :].rearrange("p b n -> p (b n)"),
                                                           scalar=up_bias[:, bass.ds(jt * H + h, 1)],
                                                           in1=fifth_v[:, q, bass.ds(sign[h], IB)],
                                                           op0=ALU.add, op1=ALU.max).then_inc(score_ready, 1)
                            if h == 1:
                                dve.wait_ge(adj_arrived[1 - q], ib * (8 * NT) + jj * 16 + 16 * (1 + q))
                                dve.wait_ge(abs_ready, k + 1)
                                dve.wait_ge(lo_ready, k + 1)
                                no_edges(k + 1, 1 - q)
                            if h == 3:
                                masked(k + 1, 1 - q)
                            if h == 5:
                                rest(k + 1, 1 - q)
                            if h == 7:
                                negative(k + 1, 1 - q)

            def check(n, z, tmp):
                link(nc.vector.tensor_scalar(tmp, z, Z_LOW, None, ALU.is_ge))
                link(nc.vector.scalar_tensor_tensor(out=tmp, in0=z, scalar=Z_HIGH, in1=tmp, op0=ALU.is_le, op1=ALU.mult))
                link(nc.vector.tensor_reduce(out_of_range[:, n, 0:1], tmp, AX.X, ALU.min))
                nc.vector.tensor_scalar(out_of_range[:, n, 0:1], out_of_range[:, n, 0:1], -1.0, 1.0, ALU.mult, ALU.add).then_inc(bad_ready[n], 1)

            def exact(n):
                edge_op = (ALU.is_gt, ALU.not_equal)[n]
                no_edge_op = (ALU.is_le, ALU.is_equal)[n]
                opening, first, second, closing = ((4, 6, 8, 0), (2, 4, 6, TB + 3))[n]
                per_unit = opening + NT * (first + second) + closing
                dve.sem_inc(x_adj_used[n], 1)
                with dve.Fori(0, NB) as ib:
                    with dve.Fori(0, XH[n]) as h:
                        u = ib * XH[n] + h
                        count = [u * per_unit, 0]

                        def xtick(ins):
                            count[1] += 1
                            ins.then_inc(x_vec[n], 1)

                        def xsettle():
                            dve.wait_ge(x_vec[n], count[0] + count[1])

                        def xlink(ins):
                            xtick(ins)
                            xsettle()

                        def logits(jt):
                            if n == 0:
                                xlink(nc.vector.scalar_tensor_tensor(out=logit_x, in0=adj_in[:, 0, :], scalar=edge_sb[:, 0, bass.ds(h, 1)],
                                                                     in1=row_x, op0=ALU.mult, op1=ALU.add))
                                xlink(nc.vector.tensor_scalar(logit_x, logit_x, d_all[:, bass.ds(jt * H + h, 1)], None, ALU.add))
                                xlink(nc.vector.scalar_tensor_tensor(out=logit_x, in0=logit_x, scalar=ALPHA, in1=logit_x, op0=ALU.mult, op1=ALU.max))
                            else:
                                xlink(nc.vector.tensor_scalar(logit_x, adj_in[:, 0, :], stat[:, 4, bass.ds(jt, 1)], None, ALU.mult))
                            xlink(nc.vector.tensor_scalar(masked_x, adj_in[:, 0, :], 0.0, MASKED, no_edge_op, ALU.mult))
                            xlink(nc.vector.tensor_tensor(logit_x, logit_x, masked_x, ALU.add))

                        if n == 0:
                            dve.wait_ge(x_rows_in, u * 32 + 32)
                            xlink(nc.vector.tensor_tensor(row_x, row_x, row_rest, ALU.add))
                            xlink(nc.vector.tensor_scalar(row_x, row_x, w_abs[:, bass.ds(h, 1)], 1.0 / (1.0 - ALPHA), ALU.mult, ALU.mult))
                        xlink(nc.vector.memset(top_x, MASKED))
                        if n == 0:
                            dve.wait_ge(x_sums_out, u * 16 + 16)
                        xtick(nc.vector.memset(acc_x[n], 0.0))
                        assert count[1] == opening
                        with dve.Fori(0, NT) as jt:
                            count[0], count[1] = u * per_unit + jt * first, opening
                            xsettle()
                            dve.wait_ge(x_adj_in[n], u * (32 * NT) + jt * 16 + 16)
                            logits(jt)
                            xlink(nc.vector.tensor_tensor(top_x, top_x, logit_x, ALU.max))
                            dve.sem_inc(x_adj_used[n], 1)
                        assert count[1] == opening + first
                        dve.sem_inc(x_top_ready[n], 1)
                        for f in range(FOLDS):
                            half = P >> (f + 1)
                            dve.wait_ge(x_half_in[n], u * (16 * FOLDS) + f * 16 + 16)
                            nc.vector.tensor_tensor(top_x[0:half, :], top_x[0:half, :], fold_x[0:half, :], ALU.max).then_inc(x_top_ready[n], 1)
                            if f < FOLDS - 1:
                                dve.wait_ge(x_top_ready[n], u * (FOLDS + 1) + f + 2)
                        with dve.Fori(0, NT) as jt:
                            count[0], count[1] = u * per_unit + jt * second, opening + NT * first
                            dve.wait_ge(x_adj_in[n], u * (32 * NT) + 16 * NT + jt * 16 + 16)
                            dve.wait_ge(x_row_top_in[n], u * 16 + 16)
                            logits(jt)
                            xlink(nc.vector.tensor_tensor(logit_x, logit_x, row_top, ALU.subtract))
                            dve.sem_inc(x_logit_ready[n], 1)
                            dve.wait_ge(x_exp_ready[n], u * NT + jt + 1)
                            xlink(nc.vector.scalar_tensor_tensor(out=logit_x, in0=adj_in[:, 0, :], scalar=0.0, in1=logit_x, op0=edge_op, op1=ALU.mult))
                            dve.sem_inc(x_weight_ready[n], 1)
                            dve.wait_ge(x_mm[n], u * NT + jt + 1)
                            sums = ps[0:HP, 0:NH, :].rearrange("p b n -> p (b n)") if n == 0 else ps[:, :, 0:F + 1]
                            xlink(nc.vector.tensor_tensor(acc_x[n], acc_x[n], sums, ALU.add))
                            dve.sem_inc(x_adj_used[n], 1)
                        assert count[1] == opening + NT * first + second
                        count[0], count[1] = u * per_unit, opening + NT * (first + second)
                        if n == 1:
                            z1 = acc_x[1][:, :, F:F + 1].rearrange("p t o -> p (t o)")
                            xlink(nc.vector.tensor_scalar(z1_fix[:, :], z1, 0.0, None, ALU.is_equal))
                            xlink(nc.vector.tensor_tensor(z1_fix[:, :], z1_fix[:, :], z1, ALU.add))
                            xlink(nc.vector.reciprocal(z1_fix[:, :], z1_fix[:, :]))
                            for t in range(TB):
                                xtick(nc.vector.scalar_tensor_tensor(out=y_all[:, bass.ds(ib * IB + t * F, F)], in0=acc_x[1][:, t, 0:F],
                                                                     scalar=z1_fix[:, t:t + 1], in1=fifth[:, bass.ds(ib * (TB * XW) + t * XW, F)],
                                                                     op0=ALU.mult, op1=ALU.add))
                        assert count[1] == per_unit
                dve.wait_ge(x_vec[n], NB * XH[n] * per_unit)
                if n == 0:
                    dve.wait_ge(x_z_in, 16)
                    nc.vector.reciprocal(z_inv[:, :], z_sb[:, :]).then_inc(x_z_inv_ready, 1)

            dve.wait_ge(z_in, 16)
            nc.vector.reciprocal(z_inv[:, :], z_sb[:, :]).then_inc(z_inv_ready, 1)
            check(0, z_sb[:, :], y_all[:, 0:H * N // P])
            dve.wait_ge(any_bad_ready[0], 1)
            with nc.vector.If(any_bad(nc.vector, 0) > 0):
                dve.wait_ge(z_inv_in, NG * 16)
                exact(0)
            link(nc.vector.memset(x1[:, :, F:F + 1], 1.0))

            def tiles(v):
                return v.rearrange("p (t f) -> p t f", f=F)

            def row(n):
                return rows_sb[:, n, :].unsqueeze(1).to_broadcast([P, TC, F])

            def chunk(v, c):
                return v[:, bass.ds(c * CH, CH)]

            def y_tile(c, t):
                return y_all[:, bass.ds(c * CH + t * F, F)]

            def x1_tile(c, t):
                return fifth[:, bass.ds(c * (TC * XW) + t * XW, F)]

            def mean(n, c):
                nc.vector.tensor_reduce(ln_stat(n, 0, c), tiles(chunk(y_all, c)), AX.X, ALU.add).then_inc(mean_tick[n], 1)
                dve.wait_ge(mean_tick[n], c + 1)
                nc.vector.tensor_scalar(ln_stat(n, 0, c), ln_stat(n, 0, c), -1.0 / F, None, ALU.mult).then_inc(mean_ready[n], 1)

            def normalise(n, c, dst):
                dve.wait_ge(deviation_ready[n], c + 1)
                nc.vector.reciprocal(ln_stat(n, 2, c), ln_stat(n, 2, c)).then_inc(scale_tick[n], 1)
                dve.wait_ge(scale_tick[n], c + 1)
                for t in range(TC):
                    nc.vector.tensor_scalar(dst(c, t), y_tile(c, t), ln_stat(n, 0, c, t), ln_stat(n, 2, c, t), ALU.add, ALU.mult).then_inc(normed[n], 1)

            def sums_over_z(c):
                dve.wait_ge(spread_mm, c + 1)
                dve.wait_ge(y_mm, c + 1)
                nc.vector.tensor_tensor(agg_n[:, :, 0:CH], agg[:, :, bass.ds(c * CH, CH)], ps[:, 0:NG, :], ALU.mult).then_inc(agg_n_ready, 1)

            def projected(c):
                dve.wait_ge(y_mm, c + 2)
                nc.vector.tensor_tensor(tiles(chunk(y_all, c)), ps[:, 4, :].rearrange("p (t f) -> p t f", f=F), row(0), ALU.add).then_inc(y_ready, 1)
                dve.wait_ge(y_ready, c + 2)
                mean(0, c)

            def residual(c):
                y = chunk(y_all, c)
                dve.wait_ge(normed[0], (c + 1) * TC)
                nc.vector.tensor_tensor(tiles(y), tiles(y), row(1), ALU.mult).then_inc(res_tick, 1)
                dve.wait_ge(res_tick, c * 3 + 1)
                nc.vector.tensor_tensor(tiles(y), tiles(y), row(2), ALU.add).then_inc(res_tick, 1)
                dve.wait_ge(res_tick, c * 3 + 2)
                nc.vector.scalar_tensor_tensor(out=y, in0=y, scalar=0.0, in1=chunk(x_all, c), op0=ALU.max, op1=ALU.add).then_inc(res_tick, 1)
                dve.wait_ge(res_tick, c * 3 + 3)
                mean(1, c)

            def scores(c):
                dve.wait_ge(prod_ready, c + 1)
                nc.vector.tensor_reduce(stat[:, 4, bass.ds(c * TC, TC)], tiles(chunk(sq_all, c)), AX.X, ALU.add).then_inc(score_tick, 1)

            def finish(i, first, second, third, ahead):
                if second:
                    residual(i - 1)
                if first:
                    projected(i)
                if third:
                    scores(i - 2)
                if second:
                    normalise(1, i - 1, x1_tile)
                if ahead:
                    sums_over_z(i + 1)
                if first:
                    normalise(0, i, y_tile)

            link(nc.vector.memset(eps_col[:, :], EPS))
            dve.wait_ge(x_in, 16)
            sums_over_z(0)
            finish(0, True, False, False, True)
            finish(1, True, True, False, True)
            with dve.Fori(2, NC - 1) as i:
                finish(i, True, True, True, True)
            finish(NC - 1, True, True, True, False)
            finish(NC, False, True, True, False)
            finish(NC + 1, False, False, True, False)
            dve.wait_ge(score_tick, NC)
            nc.vector.tensor_reduce(score_top[:, 0:1], stat[:, 4, :], AX.X, ALU.max).then_inc(score_max_ready, 1)
            dve.wait_ge(score_top_ready, 1)
            nc.vector.tensor_scalar(stat[:, 5, 0:1], score_top[:, 1:2], 0.0, -1.0, ALU.max, ALU.mult).then_inc(x1_ready, 1)

            def masks(ib, jj):
                for q in range(RING):
                    k = ib * NT + jj * RING + q
                    dve.wait_ge(e_raw, k + 1)
                    nc.vector.scalar_tensor_tensor(out=e_all[:, q % ES, :], in0=ring[:, q, :], scalar=0.0, in1=e_all[:, q % ES, :],
                                                   op0=ALU.not_equal, op1=ALU.mult).then_inc(e_ready, 1)

            def pairs(v):
                return v.rearrange("p (b t) -> p b t", t=2)

            def averages(ib):
                dve.wait_ge(l1_mm, ES + ib * NT + NT)
                s = ib % 2
                z1 = ps[:, s * BS:(s + 1) * BS, 0:2 * XW].rearrange("p b (t c) -> p b t c", c=XW)[:, :, :, F]
                nc.vector.tensor_scalar(pairs(z1_fix[:, :]), z1, Z_LOW, None, ALU.is_lt).then_inc(l1_z, 1)
                nc.vector.tensor_copy(pairs(z1_all[:, ib * TB:(ib + 1) * TB]), z1).then_inc(l1_z, 1)
                dve.wait_ge(l1_z, ib * 4 + 2)
                nc.vector.tensor_tensor(pairs(z1_fix[:, :]), pairs(z1_fix[:, :]), z1, ALU.add).then_inc(l1_z, 1)
                dve.wait_ge(l1_z, ib * 4 + 3)
                nc.vector.reciprocal(z1_fix[:, :], z1_fix[:, :]).then_inc(l1_z, 1)
                dve.wait_ge(l1_z, ib * 4 + 4)
                for t in range(TB):
                    nc.vector.scalar_tensor_tensor(out=y_all[:, bass.ds(ib * IB + t * F, F)], in0=sums1(s, t)[:, 0:F], scalar=z1_fix[:, t:t + 1],
                                                   in1=fifth[:, bass.ds(ib * (TB * XW) + t * XW, F)], op0=ALU.mult, op1=ALU.add).then_inc(l1_out, 1)

            with dve.Fori(0, NT // RING) as jj:
                masks(0, jj)
            for ib in range(1, NB):
                masks(ib, 0)
                averages(ib - 1)
                dve.wait_ge(l1_out, 1 + TB + ib * TB)
                for n in range(BC):
                    mean(2, ib * BC - BC + n)
                with dve.Fori(1, 3) as jj:
                    masks(ib, jj)
                for n in range(BC):
                    normalise(2, ib * BC - BC + n, y_tile)
                with dve.Fori(3, NT // RING) as jj:
                    masks(ib, jj)
            averages(NB - 1)
            dve.wait_ge(l1_out, 1 + TB + NB * TB)
            for c in range(NC - BC, NC):
                mean(2, c)
            check(1, z1_all[:, :], z1_tmp[:, :])
            for c in range(NC - BC, NC):
                normalise(2, c, y_tile)
            dve.wait_ge(any_bad_ready[1], 1)
            with nc.vector.If(any_bad(nc.vector, 1) > 0):
                dve.wait_ge(stored, NC * 16)
                exact(1)
                mean(3, 0)
                mean(3, 1)
                with dve.Fori(2, NC) as c:
                    mean(3, c)
                    normalise(3, c - 2, y_tile)
                normalise(3, NC - 2, y_tile)
                normalise(3, NC - 1, y_tile)


def kernel(x, adj, L0_gnn_W, L0_gnn_attn_src, L0_gnn_attn_dst, L0_gnn_edge_W, L0_gnn_edge_b, L0_gnn_fuse_W,
           L0_gnn_fuse_b, L0_gnn_ln_g, L0_gnn_ln_b, L1_gnn_H_v):
    import numpy as np
    import concourse.bacc as bacc
    from concourse import mybir as _mybir
    from concourse.bass_utils import run_bass_kernel_spmd

    x, adj, w, fuse_w = (np.asarray(a) for a in (x, adj, L0_gnn_W, L0_gnn_fuse_W))
    adj_t = adj.T.reshape(NT, P, NB, IB).transpose(2, 0, 1, 3).reshape(NB * NT * P, IB)
    attn = np.zeros((F, 2 * H), x.dtype)
    for h in range(H):
        attn[h * D:(h + 1) * D, h] = np.asarray(L0_gnn_attn_src)[h]
        attn[h * D:(h + 1) * D, H + h] = np.asarray(L0_gnn_attn_dst)[h]
    fuse = np.zeros((HG, HP, NG, F), x.dtype)
    fuse[:, 0:D] = fuse_w.T.reshape(NG, HG, D, F).transpose(1, 2, 0, 3)
    select = np.zeros((P, P), x.dtype)
    for c in range(HG):
        select[c * HP + D, c * HP:(c + 1) * HP] = 1.0
    rows = np.stack([np.asarray(a).reshape(F) for a in (L0_gnn_fuse_b, L0_gnn_ln_g, L0_gnn_ln_b, L1_gnn_H_v)])
    edge = np.stack([np.asarray(L0_gnn_edge_W).reshape(H), np.asarray(L0_gnn_edge_b).reshape(H)])
    edge_col = np.zeros((HP + H, 2), x.dtype)
    edge_col[0:H] = edge_col[HP:HP + H] = edge.T
    pick = np.zeros((P, H, P), x.dtype)
    for h in range(H):
        pick[h, h] = pick[HP + h, h] = 1.0
    arrays = {"xT": x.T, "x": x, "adjT": adj_t, "wT": w.T, "w": w, "attn": attn, "edge": edge, "edge_col": edge_col,
              "fuse": fuse.reshape(P, NG, F), "rows": rows, "select": select,
              "pick": pick, "ident": np.eye(P, dtype=x.dtype)}
    arrays = {n: np.ascontiguousarray(a) for n, a in arrays.items()}
    nc = bacc.Bacc("TRN2", target_bir_lowering=False, num_devices=1)
    args = [nc.dram_tensor(n, a.shape, _mybir.dt.from_np(a.dtype), kind="ExternalInput").ap() for n, a in arrays.items()]
    args.append(nc.dram_tensor("out", x.shape, _mybir.dt.from_np(x.dtype), kind="ExternalOutput").ap())
    gnn_kernel(nc, *args)
    return run_bass_kernel_spmd(nc, [arrays], core_ids=[0]).results[0]["out"]
```
